# Optimizing a Trainium2 kernel written in Bass

```python
import numpy as np
import jax
import jax.numpy as jnp

def _softmax(x, axis=-1):
    return jax.nn.softmax(x, axis=axis)

def _gelu(x):
    return jax.nn.gelu(x, approximate=True)

def _silu(x):
    return jax.nn.silu(x)

def _sigmoid(x):
    return jax.nn.sigmoid(x)

def _layernorm(x, axis=-1, eps=1e-05):
    m = jnp.mean(x, axis=axis, keepdims=True)
    v = jnp.var(x, axis=axis, keepdims=True)
    return (x - m) / jnp.sqrt(v + eps)

def _scatter_add(tgt, idx, src, axis=0):
    return tgt.at[idx].add(src)

def _segment_sum(src, seg, n):
    return jax.ops.segment_sum(src, seg, n)
kernel_name = 'mk_seq_preln_d1_jaxref_r4_fe9ed5'

def setup_inputs(seed: int=0):
    np.random.seed(seed)
    _w = jnp.asarray

    def _L0_attn_setup():
        import jax, jax.numpy as jnp
        import numpy as np
        MODEL_DIM = 256
        NUM_HEADS = 16
        HEAD_DIM = MODEL_DIM // NUM_HEADS
        WINDOW_SIZE = 64
        BATCH = 1
        SEQ_LEN = 1024

        def local_causal_bias(seq_len, window_size, dtype):
            i = jnp.arange(seq_len)[:, None]
            j = jnp.arange(seq_len)[None, :]
            allowed = (j <= i) & (j > i - window_size)
            neg_inf = jnp.array(-jnp.inf, dtype=dtype)
            return jnp.where(allowed, jnp.array(0.0, dtype=dtype), neg_inf)
        key = jax.random.key(seed)
        k_h, k_q, k_k, k_v, k_o = jax.random.split(key, 5)
        s = 1.0 / np.sqrt(MODEL_DIM)
        hidden = jax.random.normal(k_h, (BATCH, SEQ_LEN, MODEL_DIM), dtype=jnp.float32)
        Wq = jax.random.normal(k_q, (MODEL_DIM, MODEL_DIM), dtype=jnp.float32) * s
        Wk = jax.random.normal(k_k, (MODEL_DIM, MODEL_DIM), dtype=jnp.float32) * s
        Wv = jax.random.normal(k_v, (MODEL_DIM, MODEL_DIM), dtype=jnp.float32) * s
        Wo = jax.random.normal(k_o, (MODEL_DIM, MODEL_DIM), dtype=jnp.float32) * s
        return {'hidden': hidden, 'Wq': Wq, 'Wk': Wk, 'Wv': Wv, 'Wo': Wo}
    _L0_attn_in = _L0_attn_setup()

    def _L0_ffn_setup():
        import jax, jax.numpy as jnp
        import numpy as np
        EPS = 1e-05

        def _quantize(W):
            gamma = jnp.mean(jnp.abs(W))
            return jnp.clip(jnp.round(W / (gamma + EPS)), -1.0, 1.0)
        key = jax.random.key(seed)
        k_x, k_w1, k_b1, k_w2, k_b2 = jax.random.split(key, 5)
        n_embd = 256
        d_ff = 4 * n_embd
        B, S = (4, 1024)
        bound1 = 1.0 / np.sqrt(n_embd)
        bound2 = 1.0 / np.sqrt(d_ff)
        x = jax.random.normal(k_x, (B, S, n_embd), dtype=jnp.float32)
        W1 = jax.random.uniform(k_w1, (d_ff, n_embd), jnp.float32, -bound1, bound1)
        b1 = jax.random.uniform(k_b1, (d_ff,), jnp.float32, -bound1, bound1)
        W2 = jax.random.uniform(k_w2, (n_embd, d_ff), jnp.float32, -bound2, bound2)
        b2 = jax.random.uniform(k_b2, (n_embd,), jnp.float32, -bound2, bound2)
        return {'x': x, 'W1': W1, 'b1': b1, 'W2': W2, 'b2': b2}
    _L0_ffn_in = _L0_ffn_setup()
    _d = {'L0_attn_hidden': _L0_attn_in['hidden'], 'L0_attn_Wq': _L0_attn_in['Wq'], 'L0_attn_Wk': _L0_attn_in['Wk'], 'L0_attn_Wv': _L0_attn_in['Wv'], 'L0_attn_Wo': _L0_attn_in['Wo'], 'L0_ffn_W1': _L0_ffn_in['W1'], 'L0_ffn_b1': _L0_ffn_in['b1'], 'L0_ffn_W2': _L0_ffn_in['W2'], 'L0_ffn_b2': _L0_ffn_in['b2']}
    _x0 = _d['L0_attn_hidden']
    _d['L0_attn_hidden'] = jax.random.normal(jax.random.fold_in(jax.random.key(seed), 1), (4, 2048, 256), dtype=_x0.dtype)
    del _x0
    return _d

def reference(L0_attn_hidden, L0_attn_Wq, L0_attn_Wk, L0_attn_Wv, L0_attn_Wo, L0_ffn_W1, L0_ffn_b1, L0_ffn_W2, L0_ffn_b2):

    def _L0_attn_ref(hidden, Wq, Wk, Wv, Wo):
        import jax, jax.numpy as jnp
        import numpy as np
        MODEL_DIM = 256
        NUM_HEADS = 16
        HEAD_DIM = MODEL_DIM // NUM_HEADS
        WINDOW_SIZE = 64
        BATCH = 1
        SEQ_LEN = 1024

        def local_causal_bias(seq_len, window_size, dtype):
            i = jnp.arange(seq_len)[:, None]
            j = jnp.arange(seq_len)[None, :]
            allowed = (j <= i) & (j > i - window_size)
            neg_inf = jnp.array(-jnp.inf, dtype=dtype)
            return jnp.where(allowed, jnp.array(0.0, dtype=dtype), neg_inf)
        B, S, D = hidden.shape

        def proj(x, W):
            y = jnp.einsum('bsd,ed->bse', x, W)
            return y.reshape(B, S, NUM_HEADS, HEAD_DIM).transpose(0, 2, 1, 3)
        q = proj(hidden, Wq)
        k = proj(hidden, Wk)
        v = proj(hidden, Wv)
        scale = 1.0 / np.sqrt(HEAD_DIM)
        bias = local_causal_bias(S, WINDOW_SIZE, hidden.dtype)
        scores = jnp.einsum('bhqd,bhkd->bhqk', q, k) * scale + bias
        attn = jax.nn.softmax(scores, axis=-1)
        out = jnp.einsum('bhqk,bhkd->bhqd', attn, v)
        out = out.transpose(0, 2, 1, 3).reshape(B, S, D)
        return jnp.einsum('bsd,ed->bse', out, Wo)

    def _L0_ffn_ref(x, W1, b1, W2, b2):
        import jax, jax.numpy as jnp
        import numpy as np
        EPS = 1e-05

        def _quantize(W):
            gamma = jnp.mean(jnp.abs(W))
            return jnp.clip(jnp.round(W / (gamma + EPS)), -1.0, 1.0)
        Wq1 = _quantize(W1)
        Wq2 = _quantize(W2)
        h = jax.nn.relu(jnp.einsum('bsd,fd->bsf', x, Wq1) + b1)
        out = jnp.einsum('bsf,df->bsd', h, Wq2) + b2
        return out
    x = L0_attn_hidden
    x = x + _L0_attn_ref(_layernorm(x, axis=-1), L0_attn_Wq, L0_attn_Wk, L0_attn_Wv, L0_attn_Wo)
    x = x + _L0_ffn_ref(_layernorm(x, axis=-1), L0_ffn_W1, L0_ffn_b1, L0_ffn_W2, L0_ffn_b2)
    return x

_drawn_inputs = setup_inputs


def setup_inputs(seed=0):
    import zlib

    import numpy as np

    out = dict(_drawn_inputs(seed))
    spreads = {}
    factors = {'L0_ffn_b1': 22.137, 'L0_ffn_b2': 64.0}
    for name, (base, spread) in spreads.items():
        noise = np.random.default_rng([zlib.crc32(name.encode()), seed]).standard_normal(out[name].shape)
        drawn = base * np.exp(spread * noise) if base else spread * noise
        out[name] = jnp.asarray(drawn.astype(out[name].dtype))
    for name, factor in factors.items():
        out[name] = (out[name] * factor).astype(out[name].dtype)
    return out
```

```python
import concourse.bass as bass
from concourse import mybir
from contextlib import ExitStack


TOK, D, F = 8192, 256, 1024
CH = 512
NCH = TOK // CH
PER_BATCH = 2048 // CH
NQ = NCH * 16
NEG = -1e30


class Queue:

    def __init__(self, sem):
        self.sem, self.ops, self.count, self.seen = sem, [], 0, {}

    def do(self, fn, after=(), signal=True):
        waits = []
        for tok in after:
            if tok is None:
                continue
            sem, value = tok
            if self.seen.get(id(sem), 0) < value:
                self.seen[id(sem)] = value
                waits.append((sem, value))
        if signal:
            self.count += 1
        self.ops.append((waits, fn, (self.sem, 1) if signal else None))
        return (self.sem, self.count) if signal else None

    def dma(self, fn, sem, after=()):
        waits = []
        for tok in after:
            if tok is None:
                continue
            s, value = tok
            if self.seen.get(id(s), 0) < value:
                self.seen[id(s)] = value
                waits.append((s, value))
        self.ops.append((waits, fn, (sem, 16)))

    def wait(self, tok):
        self.ops.append(([tok], None, None))

    def emit(self, eng):
        for waits, fn, inc in self.ops:
            for sem, value in waits:
                eng.wait_ge(sem, value)
            if fn is not None:
                ins = fn(eng)
                if inc is not None:
                    ins.then_inc(inc[0], inc[1])


class Ring:

    def __init__(self, bufs):
        self.bufs, self.n, self.freed = bufs, 0, [()] * len(bufs)

    def take(self):
        i = self.n % len(self.bufs)
        self.n += 1
        return i, self.bufs[i], self.freed[i]

    def free(self, i, *toks):
        self.freed[i] = toks


def build(nc, x_d, wq_d, wk_d, wv_d, wo_d, w1_d, b1_d, w2_d, b2_d, identf_d, mask_d, maskf_d, lorow_d, out_d):
    f32, f32r, f16, b16 = mybir.dt.float32, mybir.dt.float32r, mybir.dt.float16, mybir.dt.bfloat16
    ALU, ACT, AX = mybir.AluOpType, mybir.ActivationFunctionType, mybir.AxisListType

    x_t = x_d.rearrange("b s d -> (b s) d").rearrange("(c t p) d -> c p t d", p=128, t=4)
    out_t = out_d.rearrange("b s d -> (b s) d").rearrange("(c t p) d -> c p t d", p=128, t=4)

    with ExitStack() as ctx:
        def sb(name, shape, dt):
            return ctx.enter_context(nc.sbuf_tensor(name, shape, dt))

        def sem(name):
            return ctx.enter_context(nc.semaphore(name))

        PE, DVE, SC, PL, SP = (Queue(sem(n)) for n in ("s_pe", "s_dve", "s_act", "s_pool", "s_sp"))

        identf = sb("identf", [128, 128], f32)
        identb = sb("identb", [128, 128], b16)
        mask = sb("mask", [128, 384], b16)
        maskf = sb("maskf", [128, 384], b16)
        lorow = sb("lorow", [128, 1], f32)
        mhalf = sb("mhalf", [128, 4], f32)
        onesf = sb("onesf", [128, 128], f32)
        ones = sb("ones", [64, 256], f32r)
        wT = {n: [sb(f"w{n}{p}", [128, 2, 512 if n in "qk" else 256], f32r) for p in "hl"] for n in "qkvo"}
        w1T = sb("w1T", [128, 2, F], f32r)
        w2T = sb("w2T", [128, 8, D], f32r)
        b1p = sb("b1p", [64, F], f32r)
        b2p = sb("b2p", [64, D], f32r)
        NX = 4
        xs = [sb(f"x{i}", [128, 4, D], f32) for i in range(NX)]
        xn = {s: sb(f"xn{s}", [128, t, D], f32) for s, t in (("A", 4), ("C", 2))}
        xT = {s: [sb(f"xT{s}{p}", [128, 2, 128 * t], f32r) for p in "hl"] for s, t in (("A", 4), ("C", 2))}
        st = {s: sb(f"st{s}", [128, 4, 6], f32) for s in "AC"}
        mv = {s: sb(f"mv{s}", [128, 4, 2], f32) for s in "AC"}
        ve = {s: sb(f"ve{s}", [128, 4], f32) for s in "AC"}
        rstd = {s: sb(f"rstd{s}", [128, 4], f32) for s in "AC"}
        qtmp = sb("qtmp", [128, CH], f16)
        qs = [sb(f"qs{i}", [128, 4, CH], f16) for i in range(2)]
        qbd = [sb(f"qbd{i}", [128, 16, 4, 32], f16) for i in range(2)]
        kh = [sb(f"kh{i}", [128, 4, 64 + CH], f16) for i in range(2)]
        kl = [sb(f"kl{i}", [128, 4, 64 + CH], f16) for i in range(2)]
        vd = [sb(f"vd{p}", [128, 4, 4, 4, 16], f16) for p in "hl"]
        vb = [sb(f"vb{i}", [128, 18, 4, 2, 4, 16], f16) for i in range(2)]
        pr = Ring([sb(f"p{i}", [128, 384], f32) for i in range(3)])
        pt = Ring([sb(f"pt{i}", [128, 384], f32) for i in range(2)])
        negm = Ring([sb(f"negm{i}", [128, 4], f32) for i in range(4)])
        rsum = Ring([sb(f"rsum{i}", [128, 4], f32) for i in range(4)])
        rden = Ring([sb(f"rden{i}", [128, 4], f32) for i in range(4)])
        th = [sb(f"th{i}", [128, 1600], f16) for i in range(2)]
        tl = [sb(f"tl{i}", [128, 1600], f16) for i in range(2)]
        osum = sb("osum", [128, 2, CH], f32)
        oT = [sb(f"oT{p}", [128, 2, CH], f32r) for p in "hl"]
        hT = [sb(f"hT{p}", [128, 8, CH // 2], f32r) for p in "hl"]

        banks = [ctx.enter_context(nc.psum_tensor(f"ps{i}", [128, 512], f32)) for i in range(8)]
        sring = Ring(banks[0:3])
        pvring = Ring(banks[3:4])
        wring = Ring(banks[4:8])

        s_x = [sem(f"s_x{i}") for i in range(NX)]
        s_c = sem("s_c")
        s_w = {n: sem(f"s_w{n}") for n in "qkvo12"}
        s_b = sem("s_b")
        s_out = sem("s_out")

        nat = {n: xs[2 + i // 2][:, 2 * (i % 2):2 * (i % 2) + 2, :] for i, n in enumerate("qkvo")}
        n1 = vb[0][:, 0:8].rearrange("p a b c d e -> p (a b c d e)").bitcast(f32).rearrange("p (a b) -> p a b", b=256)
        n2 = vb[1][:, 0:8].rearrange("p a b c d e -> p (a b c d e)").bitcast(f32).rearrange("p (a b) -> p a b", b=1024)
        bt = osum[0:64, :, :].rearrange("p a b -> p (a b)")
        bt2 = xn["C"][0:64, 0, :]
        bh = hT[0][0:64, :, :].rearrange("p a b -> p (a b)")
        bl = hT[1][0:64, :, :].rearrange("p a b -> p (a b)")

        x_tok = {}

        def load_x(ch, after=()):
            SP.dma(lambda e: e.dma_start(xs[ch % NX][:, :, :], x_t[ch]), s_x[ch % NX], after)
            x_tok[ch] = (s_x[ch % NX], 16 * (ch // NX + 1))

        def const(dst, src, s):
            SP.dma(lambda e: e.dma_start(dst, src), s)

        t_zero = [PL.do(lambda e: e.memset(bt, 0.0)), PL.do(lambda e: e.memset(bt2, 0.0))]
        load_x(0)
        for d, s in ((identf[:, :], identf_d), (pr.bufs[0][:, :], mask_d), (pr.bufs[1][:, :], maskf_d), (lorow[:, :], lorow_d)):
            const(d, s, s_c)
        t_const = (s_c, 16 * 4)
        for n, d in zip("qkvo", (wq_d, wk_d, wv_d, wo_d)):
            const(nat[n], d.rearrange("(t p) d -> p t d", p=128), s_w[n])
        load_x(1)
        const(n1, w1_d.rearrange("(t p) d -> p t d", p=128), s_w["1"])
        const(n2, w2_d.rearrange("(t p) f -> p t f", p=128), s_w["2"])
        for r in (0, 32):
            SP.dma(lambda e, r=r: e.dma_start(bt[r:r + 1, :], b1_d.rearrange("(a n) -> a n", a=1)), s_b, t_zero)
            SP.dma(lambda e, r=r: e.dma_start(bt2[r:r + 1, :], b2_d.rearrange("(a n) -> a n", a=1)), s_b, t_zero)
        t_bias = (s_b, 64)

        t_mhalf = DVE.do(lambda e: e.memset(mhalf[:, :], -0.5))
        t_onesf = DVE.do(lambda e: e.memset(onesf[:, :], 1.0))
        for c in range(2):
            t_ones = DVE.do(lambda e, c=c: e.tensor_copy(ones[:, 128 * c:128 * c + 128], onesf[0:64, :]), [t_onesf])
        DVE.do(lambda e: e.tensor_copy(identb[:, :], identf[:, :]), [t_const])
        DVE.do(lambda e: e.tensor_copy(mask[:, :], pr.bufs[0][:, :]))
        t_mask = DVE.do(lambda e: e.tensor_copy(maskf[:, :], pr.bufs[1][:, :]))
        for i in range(2):
            pr.free(i, t_mask)
        t_z = []
        for i in range(2):
            t_z.append(DVE.do(lambda e, i=i: e.memset(qbd[i][:, :, :, :].rearrange("p a b c -> p (a b c)").bitcast(f32), 0.0)))
        t_z.append(DVE.do(lambda e: e.memset(kh[1][:, :, :].rearrange("p a b -> p (a b)").bitcast(f32), 0.0)))
        t_z.append(DVE.do(lambda e: e.memset(kl[1][:, :, :].rearrange("p a b -> p (a b)").bitcast(f32), 0.0)))

        last = {}
        below = xn["A"][:, 0:2, :].rearrange("p a b -> p (a b)")

        def weight(n, scale):
            for t in range(2):
                i, bank, freed = wring.take()
                for c in range(2):
                    tok = PE.do(lambda e, c=c, t=t, bank=bank: e.transpose(
                        bank[:, c * 128:(c + 1) * 128], nat[n][:, c, t * 128:(t + 1) * 128], identf[:, :]),
                        [t_const, (s_w[n], 16), *freed])
                src, hd, ld = bank[:, 0:256], wT[n][0][:, t, :], wT[n][1][:, t, :]
                if n in "qk":
                    src = src.rearrange("p (h d) -> p h d", d=16).unsqueeze(2).to_broadcast([128, 16, 2, 16])
                    hd, ld = (x.rearrange("p (h v d) -> p h v d", v=2, d=16) for x in (hd, ld))
                hi = SC.do(lambda e, src=src, hd=hd: e.activation(hd, src, ACT.Copy, scale=scale), [tok])
                if scale != 1.0:
                    mul = DVE.do(lambda e, t=t, bank=bank: e.tensor_scalar(below[:, 0:256], bank[:, 0:256], scale, None, ALU.mult), [tok, hi, last.get("below")])
                    src = below[:, 0:256].rearrange("p (h d) -> p h d", d=16).unsqueeze(2).to_broadcast([128, 16, 2, 16])
                else:
                    mul = None
                lo = DVE.do(lambda e, src=src, hd=hd, ld=ld: e.tensor_tensor(ld, src, hd.bitcast(f32), ALU.subtract),
                            [tok, hi, mul])
                if mul:
                    last["below"] = lo
                wring.free(i, lo)
            return lo

        t_wt = {}
        for n, s in (("q", 0.25), ("k", 1.0), ("v", 1.0), ("o", 1.0)):
            t_wt[n] = weight(n, s)
        t_nat = t_wt["o"]

        gpart = sb("gpart", [128, 2, 8], f32)
        gsum = sb("gsum", [128, 2], f32)
        thr = sb("thr", [128, 2], f32)
        nthr = sb("nthr", [128, 2], f32)
        t_part = [
            DVE.do(lambda e: e.tensor_reduce(gpart[:, 0, :], n1, AX.X, ALU.add, apply_absolute_value=True), [(s_w["1"], 16)]),
            DVE.do(lambda e: e.tensor_reduce(gpart[:, 1, :], n2.rearrange("p a (b c) -> p (a b) c", c=256), AX.X, ALU.add,
                                             apply_absolute_value=True), [(s_w["2"], 16)])]
        t_gs = DVE.do(lambda e: e.tensor_reduce(gsum[:, :], gpart[:, :, :], AX.X, ALU.add), t_part)
        i, bank, freed = wring.take()
        t_gt = PE.do(lambda e, bank=bank: e.matmul(bank[:, 0:2], onesf[:, 0:128], gsum[:, :], start=True, stop=True),
                     [t_gs, t_onesf, *freed])
        t_thr = DVE.do(lambda e, bank=bank: e.tensor_scalar(thr[:, :], bank[:, 0:2], 1.0 / (D * F), 1e-5, ALU.mult, ALU.add), [t_gt])
        wring.free(i, t_thr)
        t_nthr = DVE.do(lambda e: e.tensor_scalar(nthr[:, :], thr[:, :], -0.5, None, ALU.mult), [t_thr])
        t_thr = DVE.do(lambda e: e.tensor_scalar(thr[:, :], thr[:, :], 0.5, None, ALU.mult), [t_nthr])

        def ternary(dst, col, sources, loaded):
            i, bank, freed = wring.take()
            for c, src in enumerate(sources):
                tok = PE.do(lambda e, c=c, src=src: e.transpose(bank[:, c * 128:(c + 1) * 128], src, identf[:, :]),
                            [t_const, loaded, *freed])
            t_b = DVE.do(lambda e: e.tensor_scalar(below[:, :], bank[:, :], nthr[:, col:col + 1], None, ALU.is_lt), [tok, t_thr, last.get("below")])
            t_q = DVE.do(lambda e: e.scalar_tensor_tensor(out=dst, in0=bank[:, :], scalar=thr[:, col:col + 1],
                                                          in1=below[:, :], op0=ALU.is_gt, op1=ALU.subtract), [t_b])
            wring.free(i, t_q)
            last["below"] = t_q
            return t_q

        for t in range(2):
            for f in range(0, 8, 4):
                t_w1 = ternary(w1T[:, t, f * 128:(f + 4) * 128], 0,
                               [n1[:, f + c, t * 128:(t + 1) * 128] for c in range(4)], (s_w["1"], 16))
        for f in range(0, 8, 2):
            t_w2 = ternary(w2T[:, f:f + 2, :].rearrange("p a b -> p (a b)"), 1,
                           [n2[:, c % 2, (f + c // 2) * 128:(f + c // 2 + 1) * 128] for c in range(4)], (s_w["2"], 16))

        t_bp = []
        for src, dst, n in ((bt, b1p, F), (bt2, b2p, D)):
            t0 = DVE.do(lambda e, dst=dst: e.memset(dst[:, :].bitcast(f32), 0.0))
            t1 = DVE.do(lambda e, src=src, n=n: e.tensor_copy(bh[:, 0:n], src), [t_bias, *t_bp])
            t2 = DVE.do(lambda e, src=src, n=n: e.tensor_tensor(bl[:, 0:n], src, bh[:, 0:n].bitcast(f32), ALU.subtract), [t1])
            DVE.do(lambda e, dst=dst, n=n: e.tensor_copy(dst[0:1, :], bh[0:1, 0:n].bitcast(f32)), [t0, t1])
            t_bp = [DVE.do(lambda e, dst=dst, n=n: e.tensor_copy(dst[32:33, :], bl[32:33, 0:n].bitcast(f32)), [t2])]

        t_z.append(DVE.do(lambda e: e.memset(vb[0][:, :].rearrange("p a b c d e -> p (a b c d e)").bitcast(f32), 0.0), [t_w1, t_part[0]]))
        t_z.append(DVE.do(lambda e: e.memset(vb[1][:, :].rearrange("p a b c d e -> p (a b c d e)").bitcast(f32), 0.0), [t_w2, t_part[1]]))
        t_init = t_z[-1]
        for ch in (2, 3):
            load_x(ch, [t_nat])


        def norm_T(s, src, nt, ready):
            toks = []
            for t in range(nt):
                a = DVE.do(lambda e, t=t: e.bn_stats(st[s][:, t, :], src[:, t, :]), [*ready, last.get("mv" + s)])
                toks.append(a)
            yield
            for t in range(nt):
                b = DVE.do(lambda e, t=t: e.bn_aggr(mv[s][:, t, :], st[s][:, t, :]), [toks[t]])
            c = PL.do(lambda e: e.tensor_scalar(ve[s][:, 0:nt], mv[s][:, 0:nt, 1], 1e-5, None, ALU.add), [b])
            c = PL.do(lambda e: e.tensor_tensor(rstd[s][:, 0:nt], ve[s][:, 0:nt], mhalf[:, 0:nt], ALU.pow), [c, t_mhalf])
            yield
            for t in range(nt):
                d = DVE.do(lambda e, t=t: e.tensor_scalar(
                    xn[s][:, t, :], src[:, t, :], mv[s][:, t, 0:1], rstd[s][:, t:t + 1], ALU.subtract, ALU.mult),
                    [c, last.get("xn" + s), t_bp[0]])
            last["mv" + s] = d
            yield
            kk = 4 // nt
            for k in range(0, 2, kk):
                i, bank, freed = wring.take()
                for j in range(kk):
                    for t in range(nt):
                        at = (j * nt + t) * 128
                        tok = PE.do(lambda e, t=t, kj=k + j, at=at, bank=bank: e.transpose(
                            bank[:, at:at + 128], xn[s][:, t, kj * 128:(kj + 1) * 128], identf[:, :]), [d, *freed])
                hd, ld = (xT[s][p][:, k:k + kk, :].rearrange("p a b -> p (a b)") for p in range(2))
                hi = SC.do(lambda e, hd=hd, bank=bank: e.activation(hd, bank[:, :], ACT.Copy),
                           [tok, last.get("xT" + s), t_bp[0]])
                lo = DVE.do(lambda e, hd=hd, ld=ld, bank=bank: e.tensor_tensor(
                    ld, bank[:, :], hd.bitcast(f32), ALU.subtract), [hi, last.get("xT" + s)])
                wring.free(i, lo)
                yield
            last["xn" + s] = tok
            last["xT" + s + "w"] = lo

        PARTS = ((0, 0), (1, 0), (0, 1))

        ready_q, ready_k, ready_v = {}, {}, {}
        s_last, pv_last, qbd_last = {}, {}, {}

        def stage_a(ch):
            b = ch % 2
            yield from norm_T("A", xs[ch % NX], 4, [x_tok[ch]])
            t_x = last["xTAw"]
            for g in range(4):
                for n in "qk":
                    i, bank, freed = wring.take()
                    m = 0
                    for wp, xp in PARTS:
                        for k in range(2):
                            lhs = wT[n][wp][:, k, 128 * g:128 * g + 128]
                            tok = PE.do(lambda e, lhs=lhs, xp=xp, k=k, m=m, bank=bank: e.matmul(
                                bank[:, :], lhs, xT["A"][xp][:, k, :], start=(m == 0), stop=(m == 5)),
                                [t_x, t_wt[n], *freed])
                            m += 1
                    if n == "q":
                        a = SC.do(lambda e, bank=bank: e.activation(qtmp[:, :], bank[:, :], ACT.Copy, scale=lorow[:, 0:1]),
                                  [tok, last.get("qtmp"), t_const])
                        d = DVE.do(lambda e, g=g, bank=bank: e.tensor_tensor(
                            qs[b][:, g, :], bank[:, :], qtmp[:, :], ALU.subtract), [a, qbd_last.get(ch - 2)])
                        last["qtmp"] = d
                        ready_q[ch, g] = d
                    else:
                        a = SC.do(lambda e, g=g, bank=bank: e.activation(kh[b][:, g, 64:], bank[:, :], ACT.Copy),
                                  [tok, s_last.get(ch - 2), last.get(("kc", ch - 1)), t_init])
                        d = DVE.do(lambda e, g=g, bank=bank: e.tensor_tensor(
                            kl[b][:, g, 64:], bank[:, :], kh[b][:, g, 64:], ALU.subtract), [a, s_last.get(ch - 2)])
                    wring.free(i, d)
                    yield
            for kk in (kh, kl):
                d = DVE.do(lambda e, kk=kk: e.tensor_copy(kk[b][:, :, 0:64], kk[1 - b][:, :, CH:CH + 64]),
                           [d, s_last.get(ch - 2), t_init])
            last["kc", ch] = d
            ready_k[ch] = d
            yield
            for u in range(2):
                i, bank, freed = wring.take()
                for t in range(2):
                    m = 0
                    for wp, xp in PARTS:
                        for k in range(2):
                            tok = PE.do(lambda e, wp=wp, xp=xp, k=k, m=m, t=t, u=u, bank=bank: e.matmul(
                                bank[:, t * 256:(t + 1) * 256],
                                xT["A"][xp][:, k, (2 * u + t) * 128:(2 * u + t + 1) * 128], wT["v"][wp][:, k, :],
                                start=(m == 0), stop=(m == 5)), [t_x, t_wt["v"], *freed])
                            m += 1
                hi_v = vd[0][:, 2 * u:2 * u + 2].rearrange("p t g h d -> p (t g h d)")
                lo_v = vd[1][:, 2 * u:2 * u + 2].rearrange("p t g h d -> p (t g h d)")
                a = SC.do(lambda e, hi_v=hi_v, bank=bank: e.activation(hi_v, bank[:, :], ACT.Copy), [tok, last.get("vd")])
                d = DVE.do(lambda e, hi_v=hi_v, lo_v=lo_v, bank=bank: e.tensor_tensor(lo_v, bank[:, :], hi_v, ALU.subtract),
                           [a, last.get("vd")])
                wring.free(i, d)
                yield
            last["xTA"] = tok
            pa = pv_last.get(ch - 2)
            t_c = DVE.do(lambda e: e.tensor_copy(vb[b][:, 0:2].rearrange("p c g v h d -> p (c g v h d)"),
                                                 vb[1 - b][:, 16:18].rearrange("p c g v h d -> p (c g v h d)")),
                         [pa, t_init, last.get("vs1")])
            last["vc"] = t_c
            n = 0
            for half in range(2):
                for c in range(4):
                    for h in range(4):
                        eng, key = (DVE, "vs0") if n % 2 else (SC, "vs1")
                        dst = vb[b][32 * h:32 * h + 32, 2 + c:18:4, :, half, h, :]
                        src = vd[half][32 * c:32 * c + 32, :, :, h, :]
                        if eng is DVE:
                            tok = DVE.do(lambda e, dst=dst, src=src: e.tensor_copy(dst, src), [d, pa, t_init])
                        else:
                            tok = SC.do(lambda e, dst=dst, src=src: e.activation(dst, src, ACT.Copy), [d, pa, t_init, t_c])
                        last[key] = tok
                        n += 1
                        if n % 8 == 0:
                            yield
            t_j = DVE.do(lambda e: e.memset(gsum[:, 0:1], 0.0), [last["vs1"]])
            last["vd"] = t_j
            ready_v[ch] = t_j

        qb = Ring(qbd)
        q_buf = {}

        def build_q(ch, g):
            i, buf, freed = qb.take()
            q_buf[ch, g] = i
            for h in range(4):
                d = DVE.do(lambda e, h=h: e.tensor_copy(
                    buf[32 * h:32 * h + 32, :, h, :],
                    qs[ch % 2][32 * h:32 * h + 32, g, :].rearrange("p (a b) -> p a b", b=32)),
                    [ready_q[ch, g], t_init, *freed])
            ready_q[ch, g, "bd"] = d
            qbd_last[ch] = d

        quad = {}

        def scores(n):
            ch, g, iq = n // 16, n // 4 % 4, n % 4
            i, bank, freed = sring.take()
            q = quad[n] = {"s": i, "bank": bank}
            first = ch % PER_BATCH == 0 and iq == 0
            buf = qbd[q_buf[ch, g]]
            PE.do(lambda e: e.matmul(bank[:, 0:384], identb[:, :], (maskf if first else mask)[:, :], start=True, stop=False,
                                     skip_group_check=True), [t_mask, *freed], signal=False)
            for u in range(4):
                blk = 4 * iq + u
                for m, kk in enumerate((kh, kl)):
                    tok = PE.do(lambda e, u=u, blk=blk, kk=kk, m=m: e.matmul(
                        bank[:, 96 * u:96 * u + 96], buf[:, blk, :, :].rearrange("p h q -> p (h q)"),
                        kk[ch % 2][:, g, 32 * blk:32 * blk + 96], start=False, stop=(m == 1 and u == 3),
                        skip_group_check=True), [ready_q[ch, g, "bd"], ready_k[ch]], signal=(u == 3 and m == 1))
            q["tok"] = tok
            if iq == 3:
                qb.free(q_buf[ch, g], tok)
                s_last[ch] = tok

        def maxes(n):
            q = quad[n]
            i, nm, freed = negm.take()
            q["nm"], q["nmi"] = nm, i
            q["max"] = DVE.do(lambda e: e.tensor_reduce(
                nm[:, :], q["bank"][:, 0:384].rearrange("p (a b) -> p a b", b=96), AX.X, ALU.max, negate=True),
                [q["tok"], *freed])

        def exps(n):
            q = quad[n]
            pi, p, pf = pr.take()
            ri, r, rf = rsum.take()
            q["p"], q["pi"], q["r"], q["ri"] = p, pi, r, ri
            for u in range(4):
                tok = SC.do(lambda e, u=u: e.activation(
                    p[:, 96 * u:96 * u + 96], q["bank"][:, 96 * u:96 * u + 96], ACT.Exp, bias=q["nm"][:, u:u + 1],
                    accum_out=r[:, u:u + 1]), [q["max"], *pf, *rf], signal=(u == 3))
            q["exp"] = tok
            sring.free(q["s"], tok)
            negm.free(q["nmi"], tok)

        def normalise(n):
            q = quad[n]
            i, rd, freed = rden.take()
            a = DVE.do(lambda e: e.reciprocal(rd[:, :], q["r"][:, :]), [q["exp"], *freed])
            rsum.free(q["ri"], a)
            p3 = q["p"][:, :].rearrange("p (a b) -> p a b", b=96)
            q["norm"] = PL.do(lambda e: e.tensor_tensor(
                p3, p3, rd[:, :].unsqueeze(2).to_broadcast([128, 4, 96]), ALU.mult), [a])
            rden.free(i, q["norm"])

        def transposes(n):
            q = quad[n]
            i, t, freed = pt.take()
            q["t"], q["ti"] = t, i
            q["tr"] = DVE.do(lambda e: e.transpose(t[:, :], q["p"][:, :]), [q["norm"], *freed])
            pr.free(q["pi"], q["tr"])

        def split(n):
            q = quad[n]
            g, iq = n // 4, n % 4
            hi, lo = (x[g % 2][:, 384 * iq:384 * iq + 384] for x in (th, tl))
            a = SC.do(lambda e: e.activation(hi, q["t"][:, :], ACT.Copy), [q["tr"], last.get(("pv", g - 2))])
            q["lo"] = PL.do(lambda e: e.tensor_tensor(lo, q["t"][:, :], hi, ALU.subtract), [a, last.get(("pv", g - 2))])
            pt.free(q["ti"], q["lo"])

        def values(n):
            ch, g, gg = n // 16, n // 4 % 4, n // 4
            i, bank, freed = pvring.take()
            vbuf = vb[ch % 2]
            first = True
            for c in range(-2, 16):
                i0, i1 = max(c, 0), min(c + 3, 16)
                off, k = 64 * i0 + 32 * c + 64, i1 - i0
                lhs = vbuf[:, c + 2, g].rearrange("p v h d -> p (v h d)")
                for tt in (th, tl):
                    rhs = tt[gg % 2][:, off:off + 64 * k].rearrange("p (a b) -> p a b", b=64)[:, :, 0:32]
                    tok = PE.do(lambda e, lhs=lhs, rhs=rhs, i0=i0, i1=i1, first=first, c=c: e.matmul(
                        bank[:, 32 * i0:32 * i1], lhs, rhs, start=first, stop=(c == 15), skip_group_check=True),
                        [quad[n]["lo"], ready_v[ch], *freed])
                    first = False
            last["pv", gg] = tok
            pv_last[ch] = tok
            base = 64 * (g % 2)
            dst = osum[base:base + 64, g // 2, :]
            a = SC.do(lambda e: e.activation(dst, bank[64:128, :], ACT.Copy), [tok, last.get("osum"), t_bp[0]])
            d = DVE.do(lambda e: e.tensor_tensor(dst, bank[0:64, :], dst, ALU.add), [a])
            pvring.free(i, d)
            if g % 2:
                t = g // 2
                hi = SC.do(lambda e: e.activation(oT[0][:, t, :], osum[:, t, :], ACT.Copy), [d, last.get("oT")])
                lo = DVE.do(lambda e: e.tensor_tensor(oT[1][:, t, :], osum[:, t, :], oT[0][:, t, :].bitcast(f32), ALU.subtract),
                            [hi, last.get("oT")])
                last["osum_next"] = lo
                last["oTw", ch] = lo
                if t == 1:
                    last["osum"] = lo
            for m in range(n - 3, n + 1):
                del quad[m]

        def stage_c(ch):
            x = xs[ch % NX]
            for u in range(2):
                x2 = x[:, 2 * u:2 * u + 2, :].rearrange("p a b -> p (a b)")
                i, bank, freed = wring.take()
                for t in range(2):
                    m = 0
                    for wp, xp in PARTS:
                        for k in range(2):
                            tok = PE.do(lambda e, wp=wp, xp=xp, k=k, m=m, t=t, u=u, bank=bank: e.matmul(
                                bank[:, t * 256:(t + 1) * 256],
                                oT[xp][:, k, (2 * u + t) * 128:(2 * u + t + 1) * 128], wT["o"][wp][:, k, :],
                                start=(m == 0), stop=(m == 5)), [last["oTw", ch], t_wt["o"], *freed])
                            m += 1
                last["oT"] = tok
                d = DVE.do(lambda e, x2=x2, bank=bank: e.tensor_tensor(x2, bank[:, :], x2, ALU.add), [tok, last["mvA"]])
                wring.free(i, d)
                yield
                yield from norm_T("C", x[:, 2 * u:2 * u + 2, :], 2, [d])
                t_x = last["xTCw"]
                for f in range(0, 8, 2):
                    i, bank, freed = wring.take()
                    for j in range(2):
                        ff, o = slice((f + j) * 128, (f + j + 1) * 128), slice(j * 256, j * 256 + 256)
                        PE.do(lambda e, ff=ff, o=o, bank=bank: e.matmul(bank[:, o], b1p[:, ff], ones[:, 0:256],
                                                                        start=True, stop=False),
                              [t_bp[0], t_ones, *freed], signal=False)
                        for xp in range(2):
                            for k in range(2):
                                tok = PE.do(lambda e, ff=ff, o=o, xp=xp, k=k, bank=bank: e.matmul(
                                    bank[:, o], w1T[:, k, ff], xT["C"][xp][:, k, :],
                                    start=False, stop=(xp + k == 2)), [t_x, t_w1])
                    hd, ld = (hT[p][:, f:f + 2, :].rearrange("p a b -> p (a b)") for p in range(2))
                    a = SC.do(lambda e, hd=hd, bank=bank: e.activation(hd, bank[:, :], ACT.Relu), [tok, last.get("hT"), t_bp[0]])
                    d = DVE.do(lambda e, hd=hd, ld=ld, bank=bank: e.scalar_tensor_tensor(
                        out=ld, in0=bank[:, :], scalar=0.0, in1=hd.bitcast(f32),
                        op0=ALU.max, op1=ALU.subtract), [a, last.get("hT")])
                    wring.free(i, d)
                    yield
                last["xTC"] = tok
                t_h = d
                i, bank, freed = wring.take()
                for t in range(2):
                    o = slice(t * 256, (t + 1) * 256)
                    PE.do(lambda e, o=o, bank=bank: e.matmul(bank[:, o], ones[:, 0:128], b2p[:, :], start=True, stop=False),
                          [t_bp[0], t_ones, *freed], signal=False)
                    for f in range(8):
                        for hp in range(2):
                            tok = PE.do(lambda e, t=t, o=o, f=f, hp=hp, bank=bank: e.matmul(
                                bank[:, o], hT[hp][:, f, t * 128:(t + 1) * 128], w2T[:, f, :],
                                start=False, stop=(f == 7 and hp == 1)), [t_h, t_w2])
                    if t == 0:
                        yield
                last["hT"] = tok
                d = DVE.do(lambda e, x2=x2, bank=bank: e.tensor_tensor(x2, bank[:, :], x2, ALU.add), [tok])
                wring.free(i, d)
                yield
            SP.dma(lambda e: e.dma_start(out_t[ch], x[:, :, :]), s_out, [d])
            if ch + NX < NCH:
                load_x(ch + NX, [(s_out, 16 * (ch + 1))])

        for _ in stage_a(0):
            pass
        build_q(0, 0)
        a_gen, c_gens = None, []
        n = 0
        while n < NQ or c_gens or n < NQ + 12:
            ch, k = n // 16, n % 16
            if k == 0 and ch + 1 < NCH:
                a_gen = stage_a(ch + 1)
            if n < NQ:
                scores(n)
                maxes(n)
                exps(n)
            if 0 <= n - 1 < NQ:
                normalise(n - 1)
            if 0 <= n - 2 < NQ:
                transposes(n - 2)
            if 0 <= n - 3 < NQ:
                split(n - 3)
            if 0 <= n - 4 < NQ and (n - 4) % 4 == 3:
                values(n - 4)
                if (n - 4) % 16 == 15:
                    c_gens.append(stage_c((n - 4) // 16))
            for _ in range(2):
                if a_gen is not None and next(a_gen, 0) == 0:
                    a_gen = None
            for _ in range(2):
                if c_gens and next(c_gens[0], 0) == 0:
                    c_gens.pop(0)
            if n % 4 == 1 and n // 4 + 1 < NQ // 4:
                if k == 13:
                    while a_gen is not None and next(a_gen, 0) != 0:
                        pass
                    a_gen = None
                build_q((n // 4 + 1) // 4, (n // 4 + 1) % 4)
            n += 1
        SP.wait((s_out, 16 * NCH))

        block = ctx.enter_context(nc.Block())

        @block.sync
        def _(eng):
            SP.emit(eng)

        @block.gpsimd
        def _(eng):
            PL.emit(eng)

        @block.scalar
        def _(eng):
            SC.emit(eng)

        @block.vector
        def _(eng):
            DVE.emit(eng)

        @block.tensor
        def _(eng):
            PE.emit(eng)


_INS = ["L0_attn_hidden", "L0_attn_Wq", "L0_attn_Wk", "L0_attn_Wv", "L0_attn_Wo",
        "L0_ffn_W1", "L0_ffn_b1", "L0_ffn_W2", "L0_ffn_b2"]


def _constants():
    import numpy as np

    q = np.arange(128)[:, None, None] % 32
    u = np.arange(4)[None, :, None]
    k = np.arange(96)[None, None, :]
    seen = (k <= q + 64) & (k > q) & (u >= 0)
    inside = 32 * u - 64 + k >= 0
    mask = np.where(seen, 0.0, NEG).astype(np.float32).reshape(128, 384)
    maskf = np.where(seen & inside, 0.0, NEG).astype(np.float32).reshape(128, 384)
    lorow = ((np.arange(128) % 32) >= 16).astype(np.float32)[:, None]
    return {"identf": np.eye(128, dtype=np.float32), "mask": mask, "maskf": maskf, "lorow": lorow}


def kernel(**inputs):
    import numpy as np
    import concourse.bacc as bacc
    from concourse.bass_utils import run_bass_kernel_spmd

    nc = bacc.Bacc("TRN2", target_bir_lowering=False, num_devices=1)
    arrays, args = {}, []
    for name, a in [(n, inputs[n]) for n in _INS] + list(_constants().items()):
        a = np.ascontiguousarray(a)
        arrays[f"in_{name}"] = a
        args.append(nc.dram_tensor(f"in_{name}", a.shape, mybir.dt.from_np(a.dtype), kind="ExternalInput").ap())
    out = nc.dram_tensor("out", (4, 2048, 256), mybir.dt.float32, kind="ExternalOutput").ap()
    build(nc, *args, out)
    r = run_bass_kernel_spmd(nc, [arrays], core_ids=[0])
    return r.results[0]["out"]
```

```python
import concourse.bass as bass
from concourse import mybir
from contextlib import ExitStack


TOK, D, F = 8192, 256, 1024
CH = 512
NCH = TOK // CH
PER_BATCH = 2048 // CH
NQ = NCH * 16
NEG = -1e30
HOP = 1000
BONUS = 300
BONUS_A = 0
BONUS_C = 300
BONUS_V = 300
BONUS_Q = 500
BONUS_N = 1000
SPREAD = 28


class Queue:

    def __init__(self, sem, cost):
        self.sem, self.cost = sem, cost
        self.ops, self.count, self.seen = [], 0, {}
        self.time, self.done_at = 0.0, {}

    def start(self, after):
        return max([self.time] + [done(tok) + HOP for tok in after if tok is not None])

    def do(self, fn, after=(), cost=None, signal=True):
        waits = []
        for tok in after:
            if tok is not None and self.seen.get(tok[0], 0) < tok[1]:
                self.seen[tok[0]] = tok[1]
                waits.append((tok[0].sem if isinstance(tok[0], Queue) else tok[0], tok[1]))
        self.time = self.start(after) + (self.cost if cost is None else cost)
        self.ops.append((waits, fn, (self.sem, 1) if signal else None))
        if not signal:
            return None
        self.count += 1
        self.done_at[self.count] = self.time
        return self, self.count

    def dma(self, fn, sem, after=()):
        waits = []
        for tok in after:
            if tok is not None and self.seen.get(tok[0], 0) < tok[1]:
                self.seen[tok[0]] = tok[1]
                waits.append((tok[0].sem if isinstance(tok[0], Queue) else tok[0], tok[1]))
        self.ops.append((waits, fn, (sem, 16)))

    def wait(self, tok):
        self.ops.append(([tok], None, None))

    def emit(self, eng):
        for waits, fn, inc in self.ops:
            for sem, value in waits:
                eng.wait_ge(sem, value)
            if fn is not None:
                ins = fn(eng)
                if inc is not None:
                    ins.then_inc(inc[0], inc[1])


def done(tok):
    return tok[0].done_at[tok[1]] if isinstance(tok[0], Queue) else 0.0


def plan(spawned, more):
    active = []
    while True:
        moved = False
        active += [[g, None] for g in spawned]
        spawned.clear()
        for item in active:
            while item[1] is None:
                try:
                    item[1] = next(item[0])
                except StopIteration:
                    item[0] = None
                    moved = True
                    break
                if item[1] is None:
                    break
                moved = True
        active = [x for x in active if x[0] is not None]
        if spawned:
            continue
        ready = [x for x in active if x[1] is not None]
        if ready:
            best = min(ready, key=lambda x: x[1][0].start(x[1][1]) - (x[1][2] if len(x[1]) > 2 else 0))
            best[1] = None
        elif not active and not more():
            return
        elif not moved and not spawned:
            assert not active, "the plan is stuck"


class Ring:

    def __init__(self, bufs):
        self.bufs, self.n, self.freed = bufs, 0, [()] * len(bufs)

    def ready(self):
        return self.freed[self.n % len(self.bufs)] is not None

    def take(self):
        i = self.n % len(self.bufs)
        self.n += 1
        freed, self.freed[i] = self.freed[i], None
        return i, self.bufs[i], freed

    def free(self, i, *toks):
        self.freed[i] = toks


def build(nc, x_d, wq_d, wk_d, wv_d, wo_d, w1_d, b1_d, w2_d, b2_d, identf_d, mask_d, maskf_d, lorow_d, out_d):
    f32, f32r, f16, b16 = mybir.dt.float32, mybir.dt.float32r, mybir.dt.float16, mybir.dt.bfloat16
    ALU, ACT, AX = mybir.AluOpType, mybir.ActivationFunctionType, mybir.AxisListType

    x_t = x_d.rearrange("b s d -> (b s) d").rearrange("(c t p) d -> c p t d", p=128, t=4)
    out_t = out_d.rearrange("b s d -> (b s) d").rearrange("(c t p) d -> c p t d", p=128, t=4)

    with ExitStack() as ctx:
        def sb(name, shape, dt):
            return ctx.enter_context(nc.sbuf_tensor(name, shape, dt))

        def sem(name):
            return ctx.enter_context(nc.semaphore(name))

        spawned = []

        def then(eng, after, fn, bonus=0):
            def piece():
                yield eng, after, bonus
                fn()
            spawned.append(piece())

        PE, DVE, SC, PL, SP = (Queue(sem(n), c) for n, c in (
            ("s_pe", 216), ("s_dve", 600), ("s_act", 480), ("s_pool", 800), ("s_sp", 0)))

        identf = sb("identf", [128, 128], f32)
        identb = sb("identb", [128, 128], b16)
        mask = sb("mask", [128, 384], b16)
        maskf = sb("maskf", [128, 384], b16)
        lorow = sb("lorow", [128, 1], f32)
        mhalf = sb("mhalf", [128, 4], f32)
        onesf = sb("onesf", [128, 128], f32)
        ones = sb("ones", [64, 256], f32r)
        wT = {n: [sb(f"w{n}{p}", [128, 2, 512 if n in "qk" else 256], f32r) for p in "hl"] for n in "qkvo"}
        w1T = sb("w1T", [128, 2, F], f32r)
        w2T = sb("w2T", [128, 8, D], f32r)
        b1p = sb("b1p", [64, F], f32r)
        b2p = sb("b2p", [64, D], f32r)
        NX = 4
        xs = [sb(f"x{i}", [128, 4, D], f32) for i in range(NX)]
        xn = {s: sb(f"xn{s}", [128, t, D], f32) for s, t in (("A", 4), ("C", 2))}
        xT = {s: [sb(f"xT{s}{p}", [128, 2, 128 * t], f32r) for p in "hl"] for s, t in (("A", 4), ("C", 2))}
        st = {s: sb(f"st{s}", [128, 4, 6], f32) for s in "AC"}
        mv = {s: sb(f"mv{s}", [128, 4, 2], f32) for s in "AC"}
        ve = {s: sb(f"ve{s}", [128, 4], f32) for s in "AC"}
        rstd = {s: sb(f"rstd{s}", [128, 4], f32) for s in "AC"}
        qtmp = sb("qtmp", [128, CH], f16)
        qs = [sb(f"qs{i}", [128, 4, CH], f16) for i in range(2)]
        qbd = [sb(f"qbd{i}", [128, 16, 4, 32], f16) for i in range(2)]
        kh = [sb(f"kh{i}", [128, 4, 64 + CH], f16) for i in range(2)]
        kl = [sb(f"kl{i}", [128, 4, 64 + CH], f16) for i in range(2)]
        vd = [sb(f"vd{p}", [128, 4, 4, 4, 16], f16) for p in "hl"]
        vb = [sb(f"vb{i}", [128, 18, 4, 2, 4, 16], f16) for i in range(2)]
        pr = Ring([sb(f"p{i}", [128, 384], f32) for i in range(3)])
        pt = Ring([sb(f"pt{i}", [128, 384], f32) for i in range(2)])
        negm = Ring([sb(f"negm{i}", [128, 4], f32) for i in range(4)])
        rsum = Ring([sb(f"rsum{i}", [128, 4], f32) for i in range(4)])
        rden = Ring([sb(f"rden{i}", [128, 4], f32) for i in range(4)])
        th = [sb(f"th{i}", [128, 1600], f16) for i in range(2)]
        tl = [sb(f"tl{i}", [128, 1600], f16) for i in range(2)]
        osum = sb("osum", [128, 2, CH], f32)
        oT = [sb(f"oT{p}", [128, 2, CH], f32r) for p in "hl"]
        hT = [sb(f"hT{p}", [128, 8, CH // 2], f32r) for p in "hl"]

        banks = [ctx.enter_context(nc.psum_tensor(f"ps{i}", [128, 512], f32)) for i in range(8)]
        sring = Ring(banks[0:3])
        pvring = Ring(banks[3:4])
        wring = Ring(banks[4:8])

        s_x = [sem(f"s_x{i}") for i in range(NX)]
        s_c = sem("s_c")
        s_w = {n: sem(f"s_w{n}") for n in "qkvo12"}
        s_b = sem("s_b")
        s_out = sem("s_out")

        nat = {n: xs[2 + i // 2][:, 2 * (i % 2):2 * (i % 2) + 2, :] for i, n in enumerate("qkvo")}
        n1 = vb[0][:, 0:8].rearrange("p a b c d e -> p (a b c d e)").bitcast(f32).rearrange("p (a b) -> p a b", b=256)
        n2 = vb[1][:, 0:8].rearrange("p a b c d e -> p (a b c d e)").bitcast(f32).rearrange("p (a b) -> p a b", b=1024)
        bt = osum[0:64, :, :].rearrange("p a b -> p (a b)")
        bt2 = xn["C"][0:64, 0, :]
        bh = hT[0][0:64, :, :].rearrange("p a b -> p (a b)")
        bl = hT[1][0:64, :, :].rearrange("p a b -> p (a b)")

        x_tok = {}

        def load_x(ch, after=()):
            SP.dma(lambda e: e.dma_start(xs[ch % NX][:, :, :], x_t[ch]), s_x[ch % NX], after)
            x_tok[ch] = (s_x[ch % NX], 16 * (ch // NX + 1))

        def const(dst, src, s):
            SP.dma(lambda e: e.dma_start(dst, src), s)

        t_zero = [PL.do(lambda e: e.memset(bt, 0.0)), PL.do(lambda e: e.memset(bt2, 0.0))]
        load_x(0)
        for d, s in ((identf[:, :], identf_d), (pr.bufs[0][:, :], mask_d), (pr.bufs[1][:, :], maskf_d), (lorow[:, :], lorow_d)):
            const(d, s, s_c)
        t_const = (s_c, 16 * 4)
        for n, d in zip("qkvo", (wq_d, wk_d, wv_d, wo_d)):
            const(nat[n], d.rearrange("(t p) d -> p t d", p=128), s_w[n])
        load_x(1)
        const(n1, w1_d.rearrange("(t p) d -> p t d", p=128), s_w["1"])
        const(n2, w2_d.rearrange("(t p) f -> p t f", p=128), s_w["2"])
        for r in (0, 32):
            SP.dma(lambda e, r=r: e.dma_start(bt[r:r + 1, :], b1_d.rearrange("(a n) -> a n", a=1)), s_b, t_zero)
            SP.dma(lambda e, r=r: e.dma_start(bt2[r:r + 1, :], b2_d.rearrange("(a n) -> a n", a=1)), s_b, t_zero)
        t_bias = (s_b, 64)

        t_mhalf = DVE.do(lambda e: e.memset(mhalf[:, :], -0.5))
        t_onesf = DVE.do(lambda e: e.memset(onesf[:, :], 1.0))
        for c in range(2):
            t_ones = DVE.do(lambda e, c=c: e.tensor_copy(ones[:, 128 * c:128 * c + 128], onesf[0:64, :]), [t_onesf])
        DVE.do(lambda e: e.tensor_copy(identb[:, :], identf[:, :]), [t_const])
        DVE.do(lambda e: e.tensor_copy(mask[:, :], pr.bufs[0][:, :]))
        t_mask = DVE.do(lambda e: e.tensor_copy(maskf[:, :], pr.bufs[1][:, :]))
        for i in range(2):
            pr.free(i, t_mask)
        t_z = []
        for i in range(2):
            t_z.append(DVE.do(lambda e, i=i: e.memset(qbd[i][:, :, :, :].rearrange("p a b c -> p (a b c)").bitcast(f32), 0.0)))
        t_z.append(DVE.do(lambda e: e.memset(kh[1][:, :, :].rearrange("p a b -> p (a b)").bitcast(f32), 0.0)))
        t_z.append(DVE.do(lambda e: e.memset(kl[1][:, :, :].rearrange("p a b -> p (a b)").bitcast(f32), 0.0)))

        last = {}
        below = xn["A"][:, 0:2, :].rearrange("p a b -> p (a b)")

        def weight(n, scale):
            for t in range(2):
                i, bank, freed = wring.take()
                for c in range(2):
                    tok = PE.do(lambda e, c=c, t=t, bank=bank: e.transpose(
                        bank[:, c * 128:(c + 1) * 128], nat[n][:, c, t * 128:(t + 1) * 128], identf[:, :]),
                        [t_const, (s_w[n], 16), *freed])
                src, hd, ld = bank[:, 0:256], wT[n][0][:, t, :], wT[n][1][:, t, :]
                if n in "qk":
                    src = src.rearrange("p (h d) -> p h d", d=16).unsqueeze(2).to_broadcast([128, 16, 2, 16])
                    hd, ld = (x.rearrange("p (h v d) -> p h v d", v=2, d=16) for x in (hd, ld))
                hi = SC.do(lambda e, src=src, hd=hd: e.activation(hd, src, ACT.Copy, scale=scale), [tok])
                if scale != 1.0:
                    mul = DVE.do(lambda e, t=t, bank=bank: e.tensor_scalar(below[:, 0:256], bank[:, 0:256], scale, None, ALU.mult), [tok, hi, last.get("below")])
                    src = below[:, 0:256].rearrange("p (h d) -> p h d", d=16).unsqueeze(2).to_broadcast([128, 16, 2, 16])
                else:
                    mul = None
                lo = DVE.do(lambda e, src=src, hd=hd, ld=ld: e.tensor_tensor(ld, src, hd.bitcast(f32), ALU.subtract),
                            [tok, hi, mul])
                if mul:
                    last["below"] = lo
                wring.free(i, lo)
            return lo

        t_wt = {}
        for n, s in (("q", 0.25), ("k", 1.0), ("v", 1.0), ("o", 1.0)):
            t_wt[n] = weight(n, s)
        t_nat = t_wt["o"]

        gpart = sb("gpart", [128, 2, 8], f32)
        gsum = sb("gsum", [128, 2], f32)
        thr = sb("thr", [128, 2], f32)
        nthr = sb("nthr", [128, 2], f32)
        t_part = [
            DVE.do(lambda e: e.tensor_reduce(gpart[:, 0, :], n1, AX.X, ALU.add, apply_absolute_value=True), [(s_w["1"], 16)]),
            DVE.do(lambda e: e.tensor_reduce(gpart[:, 1, :], n2.rearrange("p a (b c) -> p (a b) c", c=256), AX.X, ALU.add,
                                             apply_absolute_value=True), [(s_w["2"], 16)])]
        t_gs = DVE.do(lambda e: e.tensor_reduce(gsum[:, :], gpart[:, :, :], AX.X, ALU.add), t_part)
        i, bank, freed = wring.take()
        t_gt = PE.do(lambda e, bank=bank: e.matmul(bank[:, 0:2], onesf[:, 0:128], gsum[:, :], start=True, stop=True),
                     [t_gs, t_onesf, *freed])
        t_thr = DVE.do(lambda e, bank=bank: e.tensor_scalar(thr[:, :], bank[:, 0:2], 1.0 / (D * F), 1e-5, ALU.mult, ALU.add), [t_gt])
        wring.free(i, t_thr)
        t_nthr = DVE.do(lambda e: e.tensor_scalar(nthr[:, :], thr[:, :], -0.5, None, ALU.mult), [t_thr])
        t_thr = DVE.do(lambda e: e.tensor_scalar(thr[:, :], thr[:, :], 0.5, None, ALU.mult), [t_nthr])

        def ternary(dst, col, sources, loaded):
            i, bank, freed = wring.take()
            for c, src in enumerate(sources):
                tok = PE.do(lambda e, c=c, src=src: e.transpose(bank[:, c * 128:(c + 1) * 128], src, identf[:, :]),
                            [t_const, loaded, *freed])
            t_b = DVE.do(lambda e: e.tensor_scalar(below[:, :], bank[:, :], nthr[:, col:col + 1], None, ALU.is_lt), [tok, t_thr, last.get("below")])
            t_q = DVE.do(lambda e: e.scalar_tensor_tensor(out=dst, in0=bank[:, :], scalar=thr[:, col:col + 1],
                                                          in1=below[:, :], op0=ALU.is_gt, op1=ALU.subtract), [t_b])
            wring.free(i, t_q)
            last["below"] = t_q
            return t_q

        for t in range(2):
            for f in range(0, 8, 4):
                t_w1 = ternary(w1T[:, t, f * 128:(f + 4) * 128], 0,
                               [n1[:, f + c, t * 128:(t + 1) * 128] for c in range(4)], (s_w["1"], 16))
        for f in range(0, 8, 2):
            t_w2 = ternary(w2T[:, f:f + 2, :].rearrange("p a b -> p (a b)"), 1,
                           [n2[:, c % 2, (f + c // 2) * 128:(f + c // 2 + 1) * 128] for c in range(4)], (s_w["2"], 16))

        t_bp = []
        for src, dst, n in ((bt, b1p, F), (bt2, b2p, D)):
            t0 = DVE.do(lambda e, dst=dst: e.memset(dst[:, :].bitcast(f32), 0.0))
            t1 = DVE.do(lambda e, src=src, n=n: e.tensor_copy(bh[:, 0:n], src), [t_bias, *t_bp])
            t2 = DVE.do(lambda e, src=src, n=n: e.tensor_tensor(bl[:, 0:n], src, bh[:, 0:n].bitcast(f32), ALU.subtract), [t1])
            DVE.do(lambda e, dst=dst, n=n: e.tensor_copy(dst[0:1, :], bh[0:1, 0:n].bitcast(f32)), [t0, t1])
            t_bp = [DVE.do(lambda e, dst=dst, n=n: e.tensor_copy(dst[32:33, :], bl[32:33, 0:n].bitcast(f32)), [t2])]

        t_z.append(DVE.do(lambda e: e.memset(vb[0][:, :].rearrange("p a b c d e -> p (a b c d e)").bitcast(f32), 0.0), [t_w1, t_part[0]]))
        t_z.append(DVE.do(lambda e: e.memset(vb[1][:, :].rearrange("p a b c d e -> p (a b c d e)").bitcast(f32), 0.0), [t_w2, t_part[1]]))
        t_init = t_z[-1]
        for ch in (2, 3):
            load_x(ch, [t_nat])


        def norm_T(s, src, nt, ready, bonus):
            yield DVE, [*ready, last.get("mv" + s)], bonus
            toks = [DVE.do(lambda e, t=t: e.bn_stats(st[s][:, t, :], src[:, t, :]), [*ready, last.get("mv" + s)], 335)
                    for t in range(nt)]
            yield DVE, toks, bonus
            for t in range(nt):
                b = DVE.do(lambda e, t=t: e.bn_aggr(mv[s][:, t, :], st[s][:, t, :]), [toks[t]], 75)
            yield PL, [b], bonus + BONUS_N
            c = PL.do(lambda e: e.tensor_scalar(ve[s][:, 0:nt], mv[s][:, 0:nt, 1], 1e-5, None, ALU.add), [b], 190)
            c = PL.do(lambda e: e.tensor_tensor(rstd[s][:, 0:nt], ve[s][:, 0:nt], mhalf[:, 0:nt], ALU.pow), [c, t_mhalf], 960)
            yield DVE, [c, last.get("xn" + s)], bonus
            for t in range(nt):
                d = DVE.do(lambda e, t=t: e.tensor_scalar(
                    xn[s][:, t, :], src[:, t, :], mv[s][:, t, 0:1], rstd[s][:, t:t + 1], ALU.subtract, ALU.mult),
                    [c, last.get("xn" + s), t_bp[0]], 323)
            last["mv" + s] = d
            if s == "A":
                a_done[len(a_done)] = d
            kk = 4 // nt
            parts = []
            for k in range(0, 2, kk):
                while not wring.ready():
                    yield None
                i, bank, freed = wring.take()
                yield PE, [d, *freed], bonus
                for j in range(kk):
                    for t in range(nt):
                        at = (j * nt + t) * 128
                        tok = PE.do(lambda e, t=t, kj=k + j, at=at, bank=bank: e.transpose(
                            bank[:, at:at + 128], xn[s][:, t, kj * 128:(kj + 1) * 128], identf[:, :]), [d, *freed], 109)
                hd, ld = (xT[s][p][:, k:k + kk, :].rearrange("p a b -> p (a b)") for p in range(2))
                old = last.get("xT" + s)

                def high(hd=hd, ld=ld, bank=bank, tok=tok, i=i):
                    hi = SC.do(lambda e: e.activation(hd, bank[:, :], ACT.Copy), [tok, old, t_bp[0]])

                    def low():
                        lo = DVE.do(lambda e: e.tensor_tensor(ld, bank[:, :], hd.bitcast(f32), ALU.subtract), [hi, old])
                        wring.free(i, lo)
                        parts.append(lo)
                    then(DVE, [hi, old], low, bonus)
                then(SC, [tok, old], high, bonus)
            last["xn" + s] = tok
            while len(parts) < 2 // kk:
                yield None
            last["xT" + s + "w"] = parts[-1]

        PARTS = ((0, 0), (1, 0), (0, 1))

        ready_q, ready_k, ready_v = {}, {}, {}
        s_last, pv_last, qbd_last, pv_done = {}, {}, {}, set()

        def stage_a(ch):
            b = ch % 2
            while ch not in x_tok or (ch >= 2 and (ch - 2 not in s_last or (ch - 2, 3, "bd") not in ready_q)):
                yield None
            yield from norm_T("A", xs[ch % NX], 4, [x_tok[ch]], BONUS_A)
            t_x = last["xTAw"]
            parts = []
            for g in range(4):
                for n in "qk":
                    while not wring.ready():
                        yield None
                    i, bank, freed = wring.take()
                    m = 0
                    for wp, xp in PARTS:
                        yield PE, [t_x, *freed], BONUS_A
                        for k in range(2):
                            lhs = wT[n][wp][:, k, 128 * g:128 * g + 128]
                            tok = PE.do(lambda e, lhs=lhs, xp=xp, k=k, m=m, bank=bank: e.matmul(
                                bank[:, :], lhs, xT["A"][xp][:, k, :], start=(m == 0), stop=(m == 5)),
                                [t_x, t_wt[n], *freed])
                            m += 1

                    def high(n=n, g=g, bank=bank, tok=tok, i=i):
                        if n == "q":
                            a = SC.do(lambda e: e.activation(qtmp[:, :], bank[:, :], ACT.Copy, scale=lorow[:, 0:1]),
                                      [tok, last.get("qtmp"), t_const], 570)
                        else:
                            a = SC.do(lambda e: e.activation(kh[b][:, g, 64:], bank[:, :], ACT.Copy),
                                      [tok, s_last.get(ch - 2), last.get(("kc", ch - 1)), t_init])

                        def low():
                            if n == "q":
                                d = DVE.do(lambda e: e.tensor_tensor(qs[b][:, g, :], bank[:, :], qtmp[:, :], ALU.subtract),
                                           [a, qbd_last.get(ch - 2)])
                                last["qtmp"] = d
                                ready_q[ch, g] = d
                            else:
                                d = DVE.do(lambda e: e.tensor_tensor(
                                    kl[b][:, g, 64:], bank[:, :], kh[b][:, g, 64:], ALU.subtract), [a, s_last.get(ch - 2)])
                            wring.free(i, d)
                            parts.append(d)
                        then(DVE, [a], low, BONUS_A)
                    if n == "q":
                        while g and (ch, g - 1) not in ready_q:
                            yield None
                    then(SC, [tok], high, BONUS_A)
            vparts = []
            for u in range(2):
                while not wring.ready():
                    yield None
                i, bank, freed = wring.take()
                for t in range(2):
                    m = 0
                    yield PE, [t_x, *freed], BONUS_A
                    for wp, xp in PARTS:
                        for k in range(2):
                            tok = PE.do(lambda e, wp=wp, xp=xp, k=k, m=m, t=t, u=u, bank=bank: e.matmul(
                                bank[:, t * 256:(t + 1) * 256],
                                xT["A"][xp][:, k, (2 * u + t) * 128:(2 * u + t + 1) * 128], wT["v"][wp][:, k, :],
                                start=(m == 0), stop=(m == 5)), [t_x, t_wt["v"], *freed], 109)
                            m += 1

                def high(u=u, bank=bank, tok=tok, i=i):
                    hi_v = vd[0][:, 2 * u:2 * u + 2].rearrange("p t g h d -> p (t g h d)")
                    lo_v = vd[1][:, 2 * u:2 * u + 2].rearrange("p t g h d -> p (t g h d)")
                    a = SC.do(lambda e: e.activation(hi_v, bank[:, :], ACT.Copy), [tok, last.get("vd")])

                    def low():
                        d = DVE.do(lambda e: e.tensor_tensor(lo_v, bank[:, :], hi_v, ALU.subtract), [a, last.get("vd")])
                        wring.free(i, d)
                        vparts.append(d)
                    then(DVE, [a], low, BONUS_A)
                then(SC, [tok], high, BONUS_A)
            last["xTA"] = tok
            while len(parts) < 8 or len(vparts) < 2:
                yield None
            d = parts[-1]
            yield DVE, parts, BONUS_A
            for kk in (kh, kl):
                d = DVE.do(lambda e, kk=kk: e.tensor_copy(kk[b][:, :, 0:64], kk[1 - b][:, :, CH:CH + 64]),
                           [*parts, d, s_last.get(ch - 2), t_init], 140)
            last["kc", ch] = d
            ready_k[ch] = d
            while ch >= 2 and (ch - 2, 3) not in pv_done:
                yield None
            pa = pv_last.get(ch - 2)
            yield DVE, [pa, *vparts, last.get("vs1")], BONUS_A
            t_c = DVE.do(lambda e: e.tensor_copy(vb[b][:, 0:2].rearrange("p c g v h d -> p (c g v h d)"),
                                                 vb[1 - b][:, 16:18].rearrange("p c g v h d -> p (c g v h d)")),
                         [pa, t_init, last.get("vs1")], 340)
            n = 0
            for half in range(2):
                for c in range(4):
                    for h in range(4):
                        on_dve = (n * SPREAD) // 32 != ((n + 1) * SPREAD) // 32
                        dst = vb[b][32 * h:32 * h + 32, 2 + c:18:4, :, half, h, :]
                        src = vd[half][32 * c:32 * c + 32, :, :, h, :]
                        if on_dve:
                            yield DVE, vparts, BONUS_A
                            last["vs0"] = DVE.do(lambda e, dst=dst, src=src: e.tensor_copy(dst, src), [*vparts, pa, t_init], 135)
                        else:
                            yield SC, vparts, BONUS_A
                            last["vs1"] = SC.do(lambda e, dst=dst, src=src: e.activation(dst, src, ACT.Copy),
                                                [*vparts, pa, t_init, t_c], 310)
                        n += 1
            yield DVE, [last["vs1"]], BONUS_A
            t_j = DVE.do(lambda e: e.memset(gsum[:, 0:1], 0.0), [last["vs1"]], 10)
            last["vd"] = t_j
            ready_v[ch] = t_j

        qb = Ring(qbd)
        q_buf = {}
        quad = {}

        def build_q(gg):
            ch, g = gg // 4, gg % 4
            while (ch, g) not in ready_q or not qb.ready():
                yield None
            i, buf, freed = qb.take()
            q_buf[ch, g] = i
            yield DVE, [ready_q[ch, g], *freed], BONUS_Q
            for h in range(4):
                d = DVE.do(lambda e, h=h: e.tensor_copy(
                    buf[32 * h:32 * h + 32, :, h, :],
                    qs[ch % 2][32 * h:32 * h + 32, g, :].rearrange("p (a b) -> p a b", b=32)),
                    [ready_q[ch, g], t_init, *freed], 202)
            ready_q[ch, g, "bd"] = d
            qbd_last[ch] = d

        def scores(n):
            ch, g, iq = n // 16, n // 4 % 4, n % 4
            while (ch, g, "bd") not in ready_q or ch not in ready_k or not sring.ready():
                yield None
            i, bank, freed = sring.take()
            first = ch % PER_BATCH == 0 and iq == 0
            buf = qbd[q_buf[ch, g]]
            operands = [ready_q[ch, g, "bd"], ready_k[ch]]
            yield PE, [*operands, *freed], BONUS
            PE.do(lambda e: e.matmul(bank[:, 0:384], identb[:, :], (maskf if first else mask)[:, :], start=True,
                                     stop=False, skip_group_check=True), [t_mask, *freed], 163, signal=False)
            for u in range(4):
                blk = 4 * iq + u
                for m, kk in enumerate((kh, kl)):
                    tok = PE.do(lambda e, u=u, blk=blk, kk=kk, m=m: e.matmul(
                        bank[:, 96 * u:96 * u + 96], buf[:, blk, :, :].rearrange("p h q -> p (h q)"),
                        kk[ch % 2][:, g, 32 * blk:32 * blk + 96], start=False, stop=(m == 1 and u == 3),
                        skip_group_check=True), operands, 43, signal=(u == 3 and m == 1))
            quad[n] = {"s": i, "bank": bank, "tok": tok}
            if iq == 3:
                qb.free(q_buf[ch, g], tok)
                if g == 3:
                    s_last[ch] = tok

        def softmax(n):
            while n not in quad or not (negm.ready() and pr.ready() and rsum.ready()):
                yield None
            q = quad[n]
            i, nm, freed = negm.take()
            yield DVE, [q["tok"], *freed], BONUS
            t_max = DVE.do(lambda e: e.tensor_reduce(
                nm[:, :], q["bank"][:, 0:384].rearrange("p (a b) -> p a b", b=96), AX.X, ALU.max, negate=True),
                [q["tok"], *freed], 465)
            pi, p, pf = pr.take()
            ri, r, rf = rsum.take()
            yield SC, [t_max, *pf, *rf], BONUS
            for u in range(4):
                tok = SC.do(lambda e, u=u: e.activation(
                    p[:, 96 * u:96 * u + 96], q["bank"][:, 96 * u:96 * u + 96], ACT.Exp, bias=nm[:, u:u + 1],
                    accum_out=r[:, u:u + 1]), [t_max, *pf, *rf], 317, signal=(u == 3))
            q.update(p=p, pi=pi, r=r, ri=ri, exp=tok)
            sring.free(q["s"], tok)
            negm.free(i, tok)

        def probabilities(n):
            while n not in quad or "exp" not in quad[n] or not rden.ready():
                yield None
            q = quad[n]
            i, rd, freed = rden.take()
            yield DVE, [q["exp"], *freed], BONUS
            a = DVE.do(lambda e: e.reciprocal(rd[:, :], q["r"][:, :]), [q["exp"], *freed], 94)
            rsum.free(q["ri"], a)
            p3 = q["p"][:, :].rearrange("p (a b) -> p a b", b=96)
            yield PL, [a], BONUS
            q["norm"] = PL.do(lambda e: e.tensor_tensor(
                p3, p3, rd[:, :].unsqueeze(2).to_broadcast([128, 4, 96]), ALU.mult), [a], 788)
            rden.free(i, q["norm"])

        def transposes(n):
            g, iq = n // 4, n % 4
            while n not in quad or "norm" not in quad[n] or not pt.ready():
                yield None
            q = quad[n]
            i, t, freed = pt.take()
            yield DVE, [q["norm"], *freed], BONUS
            tr = DVE.do(lambda e: e.transpose(t[:, :], q["p"][:, :]), [q["norm"], *freed], 469)
            pr.free(q["pi"], tr)
            while g >= 2 and ("pv", g - 2) not in last:
                yield None
            hi, lo = (x[g % 2][:, 384 * iq:384 * iq + 384] for x in (th, tl))
            old = last.get(("pv", g - 2))
            yield SC, [tr, old], BONUS
            a = SC.do(lambda e: e.activation(hi, t[:, :], ACT.Copy), [tr, old], 413)
            yield PL, [a, old], BONUS
            q["lo"] = PL.do(lambda e: e.tensor_tensor(lo, t[:, :], hi, ALU.subtract), [a, old], 872)
            pt.free(i, q["lo"])

        def values(gg):
            ch, g = gg // 4, gg % 4
            n = 4 * gg + 3
            while n not in quad or "lo" not in quad[n] or ch not in ready_v or not pvring.ready():
                yield None
            t_p = quad[n]["lo"]
            i, bank, freed = pvring.take()
            vbuf = vb[ch % 2]
            first = True
            for c in range(-2, 16):
                if (c + 2) % 6 == 0:
                    yield PE, [t_p, ready_v[ch], *freed], BONUS_V
                i0, i1 = max(c, 0), min(c + 3, 16)
                off, k = 64 * i0 + 32 * c + 64, i1 - i0
                lhs = vbuf[:, c + 2, g].rearrange("p v h d -> p (v h d)")
                for tt in (th, tl):
                    rhs = tt[gg % 2][:, off:off + 64 * k].rearrange("p (a b) -> p a b", b=64)[:, :, 0:32]
                    tok = PE.do(lambda e, lhs=lhs, rhs=rhs, i0=i0, i1=i1, first=first, c=c: e.matmul(
                        bank[:, 32 * i0:32 * i1], lhs, rhs, start=first, stop=(c == 15), skip_group_check=True),
                        [t_p, ready_v[ch], *freed], 43)
                    first = False
            last["pv", gg] = tok
            pv_last[ch] = tok
            pv_done.add((ch, g))
            for m in range(n - 3, n + 1):
                del quad[m]
            base = 64 * (g % 2)
            dst = osum[base:base + 64, g // 2, :]
            while ch and ("oTw", ch - 1) not in last:
                yield None
            yield SC, [tok, last.get("osum")], BONUS_V
            a = SC.do(lambda e: e.activation(dst, bank[64:128, :], ACT.Copy), [tok, last.get("osum"), t_bp[0]])
            yield DVE, [a], BONUS_V
            d = DVE.do(lambda e: e.tensor_tensor(dst, bank[0:64, :], dst, ALU.add), [a])
            pvring.free(i, d)
            if g % 2:
                t = g // 2
                while ch and ("wo", ch - 1) not in last:
                    yield None
                old = last.get(("wo", ch - 1))
                yield SC, [d, old], BONUS_V
                hi = SC.do(lambda e: e.activation(oT[0][:, t, :], osum[:, t, :], ACT.Copy), [d, old], 520)
                yield DVE, [hi], BONUS_V
                lo = DVE.do(lambda e: e.tensor_tensor(
                    oT[1][:, t, :], osum[:, t, :], oT[0][:, t, :].bitcast(f32), ALU.subtract), [hi, old])
                if t == 1:
                    last["osum"] = lo
                    last["oTw", ch] = lo

        def stage_c(ch):
            x = xs[ch % NX]
            while ("oTw", ch) not in last:
                yield None
            x2s = [x[:, 2 * u:2 * u + 2, :].rearrange("p a b -> p (a b)") for u in range(2)]
            ready = {}

            def residual(u, bank, tok, i, key):
                def add():
                    d = DVE.do(lambda e: e.tensor_tensor(x2s[u], bank[:, :], x2s[u], ALU.add), [tok, a_done[ch]])
                    wring.free(i, d)
                    ready[key, u] = d
                then(DVE, [tok], add, BONUS_C)

            for u in range(2):
                while not wring.ready():
                    yield None
                i, bank, freed = wring.take()
                for t in range(2):
                    m = 0
                    yield PE, [last["oTw", ch], *freed], BONUS_C
                    for wp, xp in PARTS:
                        for k in range(2):
                            tok = PE.do(lambda e, wp=wp, xp=xp, k=k, m=m, t=t, u=u, bank=bank: e.matmul(
                                bank[:, t * 256:(t + 1) * 256],
                                oT[xp][:, k, (2 * u + t) * 128:(2 * u + t + 1) * 128], wT["o"][wp][:, k, :],
                                start=(m == 0), stop=(m == 5)), [last["oTw", ch], t_wt["o"], *freed], 109)
                            m += 1
                residual(u, bank, tok, i, "x2")
            last["wo", ch] = tok
            for u in range(2):
                while ("x2", u) not in ready:
                    yield None
                yield from norm_T("C", x[:, 2 * u:2 * u + 2, :], 2, [ready["x2", u]], BONUS_C)
                t_x = last["xTCw"]
                hparts = []
                t_oldh = last.get("hT")
                for f in range(0, 8, 2):
                    while not wring.ready():
                        yield None
                    i, bank, freed = wring.take()
                    for j in range(2):
                        ff, o = slice((f + j) * 128, (f + j + 1) * 128), slice(j * 256, j * 256 + 256)
                        yield PE, [t_x, *freed], BONUS_C
                        PE.do(lambda e, ff=ff, o=o, bank=bank: e.matmul(bank[:, o], b1p[:, ff], ones[:, 0:256],
                                                                        start=True, stop=False),
                              [t_bp[0], t_ones, *freed], 109, signal=False)
                        for xp in range(2):
                            for k in range(2):
                                tok = PE.do(lambda e, ff=ff, o=o, xp=xp, k=k, bank=bank: e.matmul(
                                    bank[:, o], w1T[:, k, ff], xT["C"][xp][:, k, :],
                                    start=False, stop=(xp + k == 2)), [t_x, t_w1], 109)

                    def high(f=f, bank=bank, tok=tok, i=i):
                        hd, ld = (hT[p][:, f:f + 2, :].rearrange("p a b -> p (a b)") for p in range(2))
                        a = SC.do(lambda e: e.activation(hd, bank[:, :], ACT.Relu), [tok, t_oldh, t_bp[0]])

                        def low():
                            d = DVE.do(lambda e: e.scalar_tensor_tensor(
                                out=ld, in0=bank[:, :], scalar=0.0, in1=hd.bitcast(f32),
                                op0=ALU.max, op1=ALU.subtract), [a, t_oldh])
                            wring.free(i, d)
                            hparts.append(d)
                        then(DVE, [a, t_oldh], low, BONUS_C)
                    then(SC, [tok, t_oldh], high, BONUS_C)
                last["xTC"] = tok
                while len(hparts) < 4:
                    yield None
                while not wring.ready():
                    yield None
                i, bank, freed = wring.take()
                for t in range(2):
                    o = slice(t * 256, (t + 1) * 256)
                    yield PE, [*hparts, *freed], BONUS_C
                    PE.do(lambda e, o=o, bank=bank: e.matmul(bank[:, o], ones[:, 0:128], b2p[:, :], start=True, stop=False),
                          [t_bp[0], t_ones, *freed], 109, signal=False)
                    for f in range(8):
                        for hp in range(2):
                            tok = PE.do(lambda e, t=t, o=o, f=f, hp=hp, bank=bank: e.matmul(
                                bank[:, o], hT[hp][:, f, t * 128:(t + 1) * 128], w2T[:, f, :],
                                start=False, stop=(f == 7 and hp == 1)), [*hparts, t_w2], 109)
                        if f % 2 and f < 7:
                            yield PE, [], BONUS_C
                last["hT"] = tok
                residual(u, bank, tok, i, "out")
            while ("out", 1) not in ready:
                yield None
            d = ready["out", 1]
            SP.dma(lambda e: e.dma_start(out_t[ch], x[:, :, :]), s_out, [ready["out", 0], d])
            if ch + NX < NCH:
                load_x(ch + NX, [(s_out, 16 * (ch + 1))])

        a_done = {}

        def each(stage, count):
            for n in range(count):
                yield from stage(n)

        spawned += [each(scores, NQ), each(softmax, NQ), each(probabilities, NQ), each(transposes, NQ),
                    each(values, NQ // 4), each(build_q, NQ // 4), each(stage_c, NCH), each(stage_a, NCH)]
        plan(spawned, lambda: False)
        SP.wait((s_out, 16 * NCH))

        block = ctx.enter_context(nc.Block())

        @block.sync
        def _(eng):
            SP.emit(eng)

        @block.gpsimd
        def _(eng):
            PL.emit(eng)

        @block.scalar
        def _(eng):
            SC.emit(eng)

        @block.vector
        def _(eng):
            DVE.emit(eng)

        @block.tensor
        def _(eng):
            PE.emit(eng)


_INS = ["L0_attn_hidden", "L0_attn_Wq", "L0_attn_Wk", "L0_attn_Wv", "L0_attn_Wo",
        "L0_ffn_W1", "L0_ffn_b1", "L0_ffn_W2", "L0_ffn_b2"]


def _constants():
    import numpy as np

    q = np.arange(128)[:, None, None] % 32
    u = np.arange(4)[None, :, None]
    k = np.arange(96)[None, None, :]
    seen = (k <= q + 64) & (k > q) & (u >= 0)
    inside = 32 * u - 64 + k >= 0
    mask = np.where(seen, 0.0, NEG).astype(np.float32).reshape(128, 384)
    maskf = np.where(seen & inside, 0.0, NEG).astype(np.float32).reshape(128, 384)
    lorow = ((np.arange(128) % 32) >= 16).astype(np.float32)[:, None]
    return {"identf": np.eye(128, dtype=np.float32), "mask": mask, "maskf": maskf, "lorow": lorow}


def kernel(**inputs):
    import numpy as np
    import concourse.bacc as bacc
    from concourse.bass_utils import run_bass_kernel_spmd

    nc = bacc.Bacc("TRN2", target_bir_lowering=False, num_devices=1)
    arrays, args = {}, []
    for name, a in [(n, inputs[n]) for n in _INS] + list(_constants().items()):
        a = np.ascontiguousarray(a)
        arrays[f"in_{name}"] = a
        args.append(nc.dram_tensor(f"in_{name}", a.shape, mybir.dt.from_np(a.dtype), kind="ExternalInput").ap())
    out = nc.dram_tensor("out", (4, 2048, 256), mybir.dt.float32, kind="ExternalOutput").ap()
    build(nc, *args, out)
    r = run_bass_kernel_spmd(nc, [arrays], core_ids=[0])
    return r.results[0]["out"]
```

```python
import concourse.bass as bass
from concourse import mybir
from contextlib import ExitStack


TOK, D, F = 8192, 256, 1024
CH = 512
NCH = TOK // CH
PER_BATCH = 2048 // CH
NQ = NCH * 16
NEG = -1e30
HOP = 600
BONUS = 600
BONUS_V = 150
AT_K = 0.7
BONUS_N = 300
DMA_EVERY = 700
DMA_TIME = 2500
NS = 3
NP = 3
NT = 2
PACE = 1000
AT_A = -0.1
LEN_A = 0.4
AT_S = 0.9
AT_C = -0.2
LEN_C = 1.1
AT_W = -0.5
AT_B = -1
AT_G = 0
TAIL = 0
AT_T = 0.6
Q_LATER = 0.2
O_LOW_POOL = 0
ON_ACT_A = 0
ON_ACT_C = 0
SPREAD = 14
DMA_DONE = {}


class Queue:

    def __init__(self, sem, cost):
        self.sem, self.cost = sem, cost
        self.ops, self.count, self.seen = [], 0, {}
        self.time, self.done_at, self.dmas = 0.0, {}, {}

    def start(self, after):
        return max([self.time] + [done(tok) + HOP for tok in after if tok is not None])

    def do(self, fn, after=(), cost=None, signal=True):
        waits = []
        for tok in after:
            if tok is not None and self.seen.get(tok[0], 0) < tok[1]:
                self.seen[tok[0]] = tok[1]
                waits.append((tok[0].sem if isinstance(tok[0], Queue) else tok[0], tok[1]))
        self.time = self.start(after) + (self.cost if cost is None else cost)
        self.ops.append((waits, fn, (self.sem, 1) if signal else None))
        if not signal:
            return None
        self.count += 1
        self.done_at[self.count] = self.time
        return self, self.count

    def dma(self, fn, sem, after=()):
        waits = []
        for tok in after:
            if tok is not None and self.seen.get(tok[0], 0) < tok[1]:
                self.seen[tok[0]] = tok[1]
                waits.append((tok[0].sem if isinstance(tok[0], Queue) else tok[0], tok[1]))
        start = self.start(after)
        self.time = start + DMA_EVERY
        self.dmas[sem] = self.dmas.get(sem, 0) + 16
        DMA_DONE[sem, self.dmas[sem]] = start + DMA_TIME
        self.ops.append((waits, fn, (sem, 16)))
        return sem, self.dmas[sem]

    def wait(self, tok):
        self.ops.append(([tok], None, None))

    def emit(self, eng):
        for waits, fn, inc in self.ops:
            for sem, value in waits:
                eng.wait_ge(sem, value)
            if fn is not None:
                ins = fn(eng)
                if inc is not None:
                    ins.then_inc(inc[0], inc[1])


def done(tok):
    return tok[0].done_at[tok[1]] if isinstance(tok[0], Queue) else DMA_DONE.get(tok, 0.0)


def plan(spawned):
    active, still = [], 0
    while True:
        moved = False
        active += [[g, None] for g in spawned]
        spawned.clear()
        for item in active:
            while item[1] is None:
                try:
                    item[1] = next(item[0])
                except StopIteration:
                    item[0] = None
                    moved = True
                    break
                if item[1] is None:
                    break
                moved = True
        active = [x for x in active if x[0] is not None]
        if spawned:
            continue
        ready = [x for x in active if x[1] is not None]
        if ready:
            best = min(ready, key=lambda x: x[1][0].start(x[1][1]) - (x[1][2] if len(x[1]) > 2 else 0))
            best[1] = None
        elif not active:
            return
        else:
            still = 0 if moved else still + 1
            assert still < 3, "the plan is stuck"


class Ring:

    def __init__(self, bufs):
        self.bufs, self.n, self.freed = bufs, 0, [()] * len(bufs)

    def ready(self):
        return self.freed[self.n % len(self.bufs)] is not None

    def take(self):
        i = self.n % len(self.bufs)
        self.n += 1
        freed, self.freed[i] = self.freed[i], None
        return i, self.bufs[i], freed

    def free(self, i, *toks):
        self.freed[i] = toks


def build(nc, x_d, wq_d, wk_d, wv_d, wo_d, w1_d, b1_d, w2_d, b2_d, identf_d, mask_d, maskf_d, out_d):
    f32, f32r, f16, b16 = mybir.dt.float32, mybir.dt.float32r, mybir.dt.float16, mybir.dt.bfloat16
    ALU, ACT, AX = mybir.AluOpType, mybir.ActivationFunctionType, mybir.AxisListType

    x_t = x_d.rearrange("b s d -> (b s) d").rearrange("(c t p) d -> c p t d", p=128, t=4)
    out_t = out_d.rearrange("b s d -> (b s) d").rearrange("(c t p) d -> c p t d", p=128, t=4)

    with ExitStack() as ctx:
        def sb(name, shape, dt):
            return ctx.enter_context(nc.sbuf_tensor(name, shape, dt))

        def sem(name):
            return ctx.enter_context(nc.semaphore(name))

        spawned = []

        def due(position):
            return -PACE * position

        def then(eng, after, fn, bonus=0):
            def piece():
                yield eng, after, bonus
                fn()
            spawned.append(piece())

        PE, DVE, SC, PL, SP = (Queue(sem(n), c) for n, c in (
            ("s_pe", 216), ("s_dve", 600), ("s_act", 480), ("s_pool", 800), ("s_sp", 0)))

        identf = sb("identf", [128, 128], f32)
        identb = sb("identb", [128, 128], b16)
        mask = sb("mask", [128, 384], b16)
        maskf = sb("maskf", [128, 384], b16)
        mhalf = sb("mhalf", [128, 4], f32)
        onesf = sb("onesf", [128, 128], f32)
        ones = sb("ones", [64, 256], f32r)
        wT = {n: [sb(f"w{n}{p}", [128, 2, 256], f32r) for p in "hl"] for n in "qkvo"}
        w1T = sb("w1T", [128, 2, F], f32r)
        w2T = sb("w2T", [128, 8, D], f32r)
        b1p = sb("b1p", [64, F], f32r)
        b2p = sb("b2p", [64, D], f32r)
        NX = 4
        xs = [sb(f"x{i}", [128, 4, D], f32) for i in range(NX)]
        xn = {s: sb(f"xn{s}", [128, t, D], f32) for s, t in (("A", 4), ("C", 2))}
        xT = {s: [sb(f"xT{s}{p}", [128, 2, 128 * t], f32r) for p in "hl"] for s, t in (("A", 4), ("C", 2))}
        st = {s: sb(f"st{s}", [128, 4, 6], f32) for s in "AC"}
        mv = {s: sb(f"mv{s}", [128, 4, 2], f32) for s in "AC"}
        ve = {s: sb(f"ve{s}", [128, 4], f32) for s in "AC"}
        nmr = {s: sb(f"nmr{s}", [128, 4], f32) for s in "AC"}
        rstd = {s: sb(f"rstd{s}", [128, 4], f32) for s in "AC"}
        qk_stage = {n: Ring([sb(f"{n}s{i}", [128, 2, CH], f16) for i in range(2)]) for n in "qk"}
        qbd = [sb(f"qbd{g}", [128, 4 * CH], f16) for g in range(4)]
        ks = [sb(f"k{i}", [128, 2, 4, 64 + CH], f16) for i in range(2)]
        vd = sb("vd", [128, 4, 4, 2, 4, 16], f16)
        vb = [sb(f"vb{i}", [128, 18, 4, 2, 4, 16], f16) for i in range(2)]
        pr = Ring([sb(f"p{i}", [128, 384], f32) for i in range(NP)])
        pt = Ring([sb(f"pt{i}", [128, 384], f32) for i in range(NT)])
        negm = Ring([sb(f"negm{i}", [128, 4], f32) for i in range(4)])
        rsum = Ring([sb(f"rsum{i}", [128, 4], f32) for i in range(4)])
        rden = Ring([sb(f"rden{i}", [128, 4], f32) for i in range(4)])
        th = [sb(f"th{i}", [128, 1600], f16) for i in range(2)]
        tl = [sb(f"tl{i}", [128, 1600], f16) for i in range(2)]
        osum = sb("osum", [128, 2, CH], f32)
        oT = [sb(f"oT{p}", [128, 2, CH], f32r) for p in "hl"]
        hT = [sb(f"hT{p}", [128, 8, CH // 2], f32r) for p in "hl"]

        banks = [ctx.enter_context(nc.psum_tensor(f"ps{i}", [128, 512], f32)) for i in range(8)]
        sring = Ring(banks[0:NS])
        pvring = Ring(banks[NS:NS + 1])
        wring = Ring(banks[NS + 1:8])

        s_x = [sem(f"s_x{i}") for i in range(NX)]
        s_c = sem("s_c")
        s_w = {n: sem(f"s_w{n}") for n in "qkvo12"}
        s_b = sem("s_b")
        s_q = [sem(f"s_q{g}") for g in range(4)]
        s_k = [[sem(f"s_k{b}{t}") for t in range(2)] for b in range(2)]
        s_out = sem("s_out")

        nat = {n: xs[2 + i // 2][:, 2 * (i % 2):2 * (i % 2) + 2, :] for i, n in enumerate("qkvo")}
        n1 = vb[1][:, 0:8].rearrange("p a b c d e -> p (a b c d e)").bitcast(f32).rearrange("p (a b) -> p a b", b=256)
        n2 = vb[1][:, 8:16].rearrange("p a b c d e -> p (a b c d e)").bitcast(f32).rearrange("p (a b) -> p a b", b=1024)
        bt = osum[0:64, :, :].rearrange("p a b -> p (a b)")
        bt2 = xn["C"][0:64, 0, :]
        bh = oT[0][0:64, :, :].rearrange("p a b -> p (a b)")
        bl = oT[1][0:64, :, :].rearrange("p a b -> p (a b)")

        x_tok = {}

        def load_x(ch, after=()):
            SP.dma(lambda e: e.dma_start(xs[ch % NX][:, :, :], x_t[ch]), s_x[ch % NX], after)
            x_tok[ch] = (s_x[ch % NX], 16 * (ch // NX + 1))

        def const(dst, src, s):
            SP.dma(lambda e: e.dma_start(dst, src), s)

        t_zero = [PL.do(lambda e: e.memset(bt, 0.0)), PL.do(lambda e: e.memset(bt2, 0.0))]
        load_x(0)
        for d, s in ((identf[:, :], identf_d), (pr.bufs[0][:, :], mask_d), (pr.bufs[1][:, :], maskf_d)):
            const(d, s, s_c)
        t_const = (s_c, 16 * 3)
        for n, d in zip("qkvo", (wq_d, wk_d, wv_d, wo_d)):
            const(nat[n], d.rearrange("(t p) d -> p t d", p=128), s_w[n])
        load_x(1)
        const(n1, w1_d.rearrange("(t p) d -> p t d", p=128), s_w["1"])
        const(n2, w2_d.rearrange("(t p) f -> p t f", p=128), s_w["2"])
        for r in (0, 32):
            SP.dma(lambda e, r=r: e.dma_start(bt[r:r + 1, :], b1_d.rearrange("(a n) -> a n", a=1)), s_b, t_zero)
            SP.dma(lambda e, r=r: e.dma_start(bt2[r:r + 1, :], b2_d.rearrange("(a n) -> a n", a=1)), s_b, t_zero)
        t_bias = (s_b, 64)

        t_mhalf = DVE.do(lambda e: e.memset(mhalf[:, :], -0.5))
        t_onesf = DVE.do(lambda e: e.memset(onesf[:, :], 1.0))
        for c in range(2):
            t_ones = DVE.do(lambda e, c=c: e.tensor_copy(ones[:, 128 * c:128 * c + 128], onesf[0:64, :]), [t_onesf])
        DVE.do(lambda e: e.tensor_copy(identb[:, :], identf[:, :]), [t_const])
        DVE.do(lambda e: e.tensor_copy(mask[:, :], pr.bufs[0][:, :]))
        t_mask = DVE.do(lambda e: e.tensor_copy(maskf[:, :], pr.bufs[1][:, :]))
        for i in range(2):
            pr.free(i, t_mask)
        PL.do(lambda e: e.memset(ks[1][:, :, :, :].rearrange("p v a b -> p (v a b)").bitcast(f32), 0.0), cost=2000)
        for t in qbd:
            t_init = PL.do(lambda e, t=t: e.memset(t[:, :].bitcast(f32), 0.0), cost=1000)

        last = {}
        below = xn["C"][:, :, :].rearrange("p a b -> p (a b)")

        t_wt = {}

        def weight(n, scale, pos):
            for t in range(2):
                while not wring.ready():
                    yield None
                i, bank, freed = wring.take()
                yield PE, [t_const, *freed], due(pos)
                for c in range(2):
                    tok = PE.do(lambda e, c=c, t=t, bank=bank: e.transpose(
                        bank[:, c * 128:(c + 1) * 128], nat[n][:, c, t * 128:(t + 1) * 128], identf[:, :]),
                        [t_const, (s_w[n], 16), *freed])
                src, hd, ld = bank[:, 0:256], wT[n][0][:, t, :], wT[n][1][:, t, :]
                yield SC, [tok], due(pos)
                hi = SC.do(lambda e, src=src, hd=hd: e.activation(hd, src, ACT.Copy, scale=scale), [tok])
                yield DVE, [hi], due(pos)
                if scale != 1.0:
                    mul = DVE.do(lambda e, t=t, bank=bank: e.tensor_scalar(
                        below[:, 256:512], bank[:, 0:256], scale, None, ALU.mult), [tok, hi, last.get("below")])
                    src = below[:, 256:512]
                else:
                    mul = None
                lo = DVE.do(lambda e, src=src, hd=hd, ld=ld: e.tensor_tensor(ld, src, hd.bitcast(f32), ALU.subtract),
                            [tok, hi, mul])
                if mul:
                    last["below"] = lo
                wring.free(i, lo)
            t_wt[n] = lo

        gpart = sb("gpart", [128, 2, 8], f32)
        gsum = sb("gsum", [128, 2], f32)
        thr = sb("thr", [128, 2], f32)
        nthr = sb("nthr", [128, 2], f32)
        junk = sb("junk", [128, 1], f32)

        def ternary(dst, col, sources, loaded, ready):
            while not wring.ready() or "bias" not in last:
                yield None
            i, bank, freed = wring.take()
            yield PE, [t_const, *freed], due(AT_T)
            for c, src in enumerate(sources):
                tok = PE.do(lambda e, c=c, src=src: e.transpose(bank[:, c * 128:(c + 1) * 128], src, identf[:, :]),
                            [t_const, loaded, *freed], 213)
            yield DVE, [tok], due(AT_T)
            t_b = DVE.do(lambda e: e.tensor_scalar(below[:, :], bank[:, :], nthr[:, col:col + 1], None, ALU.is_lt),
                         [tok, *ready, last.get("below"), last["bias"]])
            t_q = DVE.do(lambda e: e.scalar_tensor_tensor(out=dst, in0=bank[:, :], scalar=thr[:, col:col + 1],
                                                          in1=below[:, :], op0=ALU.is_gt, op1=ALU.subtract), [t_b])
            wring.free(i, t_q)
            last["below"] = t_q

        def weights():
            for n, scale in (("q", 0.25), ("k", 1.0), ("v", 1.0)):
                yield from weight(n, scale, AT_W)

        def more_weights():
            while "v" not in t_wt:
                yield None
            yield from weight("o", 1.0, AT_B)
            for ch in (2, 3):
                def load(ch=ch):
                    load_x(ch, [t_wt["o"]])
                then(SP, [t_wt["o"]], load)
            t_bp = []
            for src, dst, n in ((bt, b1p, F), (bt2, b2p, D)):
                yield PL, [], due(AT_B)
                t0 = PL.do(lambda e, dst=dst: e.memset(dst[:, :].bitcast(f32), 0.0))
                t1 = PL.do(lambda e, src=src, n=n: e.tensor_copy(bh[:, 0:n], src), [t_bias, *t_bp])
                t2 = PL.do(lambda e, src=src, n=n: e.tensor_tensor(bl[:, 0:n], src, bh[:, 0:n].bitcast(f32), ALU.subtract), [t1])
                yield SC, [t2], due(AT_B)
                SC.do(lambda e, dst=dst, n=n: e.activation(dst[0:1, :], bh[0:1, 0:n].bitcast(f32), ACT.Copy), [t0, t2])
                t_bp = [SC.do(lambda e, dst=dst, n=n: e.activation(dst[32:33, :], bl[32:33, 0:n].bitcast(f32), ACT.Copy), [t2])]
            last["bias"] = last["wo", -1] = last["osum"] = t_bp[0]

        def ffn_weights():
            for j in range(16):
                loaded = (s_w["1" if j < 8 else "2"], 16)
                yield SC, [loaded], due(AT_G)
                junk_to = (th[0], tl[0], th[1])[j // 6][:, 256 * (j % 6):256 * (j % 6) + 256]
                w, part = (n1, n2.rearrange("p a (b c) -> p (a b) c", c=256))[j // 8][:, j % 8, :], gpart[:, j // 8, j % 8:j % 8 + 1]
                t_part = SC.do(lambda e, w=w, part=part, junk_to=junk_to: e.activation(junk_to, w, ACT.Abs, accum_out=part),
                               [loaded], 400)
            last["pv", -2] = last["pv", -1] = t_part
            yield DVE, [t_part], due(AT_T)
            t_gs = DVE.do(lambda e: e.tensor_reduce(gsum[:, :], gpart[:, :, :], AX.X, ALU.add), [t_part])
            while not wring.ready():
                yield None
            i, bank, freed = wring.take()
            yield PE, [t_gs, *freed], due(AT_T)
            t_gt = PE.do(lambda e, bank=bank: e.matmul(bank[:, 0:2], onesf[:, 0:128], gsum[:, :], start=True, stop=True),
                         [t_gs, t_onesf, *freed])
            yield DVE, [t_gt], due(AT_T)
            t_thr = DVE.do(lambda e, bank=bank: e.tensor_scalar(
                thr[:, :], bank[:, 0:2], 1.0 / (D * F), 1e-5, ALU.mult, ALU.add), [t_gt], 100)
            wring.free(i, t_thr)
            t_nthr = DVE.do(lambda e: e.tensor_scalar(nthr[:, :], thr[:, :], -0.5, None, ALU.mult), [t_thr], 100)
            t_thr = DVE.do(lambda e: e.tensor_scalar(thr[:, :], thr[:, :], 0.5, None, ALU.mult), [t_nthr], 100)
            for t in range(2):
                for f in range(0, 8, 4):
                    yield from ternary(w1T[:, t, f * 128:(f + 4) * 128], 0,
                                       [n1[:, f + c, t * 128:(t + 1) * 128] for c in range(4)], (s_w["1"], 16), [t_thr])
            for f in range(0, 8, 2):
                yield from ternary(w2T[:, f:f + 2, :].rearrange("p a b -> p (a b)"), 1,
                                   [n2[:, c % 2, (f + c // 2) * 128:(f + c // 2 + 1) * 128] for c in range(4)],
                                   (s_w["2"], 16), [t_thr])
            last["ffn"] = last["xnC"] = last["below"]

        def zero_values():
            parts = (vb[0][:, :], vb[1][:, 16:18], vb[1][:, 0:16])
            for i, t in enumerate(parts):
                while i == 2 and "ffn" not in last:
                    yield None
                after = [last["ffn"]] if i == 2 else []
                yield PL, after, due(0)
                tok = PL.do(lambda e, t=t: e.memset(
                    t.rearrange("p a b c d e -> p (a b c d e)").bitcast(f32), 0.0), after, 500 if i == 1 else 4000)
                if i:
                    last["zero", i - 1] = tok


        def norm_T(s, count, src, nt, ready, bonus):
            before = last.get("mv" + s, ())
            yield DVE, [*ready, *before], bonus
            toks = [DVE.do(lambda e, t=t: e.bn_stats(st[s][:, t, :], src[:, t, :]), [*ready, *before], 335)
                    for t in range(nt)]
            yield DVE, toks, bonus
            for t in range(nt):
                b = DVE.do(lambda e, t=t: e.bn_aggr(mv[s][:, t, :], st[s][:, t, :]), [toks[t]], 75)
            yield PL, [b], bonus + BONUS_N
            c = PL.do(lambda e: e.tensor_scalar(ve[s][:, 0:nt], mv[s][:, 0:nt, 1], 1e-5, None, ALU.add), [b], 190)
            c = PL.do(lambda e: e.tensor_tensor(rstd[s][:, 0:nt], ve[s][:, 0:nt], mhalf[:, 0:nt], ALU.pow), [c, t_mhalf], 960)
            free = [last.get("xn" + s)] + ([last["bias"]] if s == "C" else [])
            on_act = ON_ACT_A if s == "A" else ON_ACT_C
            if on_act:
                yield DVE, [c], bonus
                m = DVE.do(lambda e: e.scalar_tensor_tensor(out=nmr[s][:, 0:nt], in0=mv[s][:, 0:nt, 0], scalar=-1.0,
                                                            in1=rstd[s][:, 0:nt], op0=ALU.mult, op1=ALU.mult), [c], 70)
            normed = []
            for t in range(nt):
                if t < on_act:
                    yield SC, [m, *free], bonus
                    normed.append(SC.do(lambda e, t=t: e.activation(
                        xn[s][:, t, :], src[:, t, :], ACT.Identity, scale=rstd[s][:, t:t + 1], bias=nmr[s][:, t:t + 1]),
                        [m, *free], 400))
                else:
                    yield DVE, [c, *free], bonus
                    normed.append(DVE.do(lambda e, t=t: e.tensor_scalar(
                        xn[s][:, t, :], src[:, t, :], mv[s][:, t, 0:1], rstd[s][:, t:t + 1], ALU.subtract, ALU.mult),
                        [c, *free], 323))
            last["mv" + s] = normed
            if s == "A":
                a_done[len(a_done)] = normed
            kk = 4 // nt
            parts = []
            while count and ("xT" + s, count - 1) not in last:
                yield None
            for k in range(0, 2, kk):
                while not wring.ready():
                    yield None
                i, bank, freed = wring.take()
                yield PE, [*normed, *freed], bonus
                for j in range(kk):
                    for t in range(nt):
                        at = (j * nt + t) * 128
                        tok = PE.do(lambda e, t=t, kj=k + j, at=at, bank=bank: e.transpose(
                            bank[:, at:at + 128], xn[s][:, t, kj * 128:(kj + 1) * 128], identf[:, :]), [*normed, *freed], 109)
                hd, ld = (xT[s][p][:, k:k + kk, :].rearrange("p a b -> p (a b)") for p in range(2))
                old = last.get(("xT" + s, count - 1), last.get("xT" + s))

                def high(hd=hd, ld=ld, bank=bank, tok=tok, i=i):
                    hi = SC.do(lambda e: e.activation(hd, bank[:, :], ACT.Copy), [tok, old])

                    def low():
                        lo = DVE.do(lambda e: e.tensor_tensor(ld, bank[:, :], hd.bitcast(f32), ALU.subtract), [hi, old])
                        wring.free(i, lo)
                        parts.append(lo)
                    then(DVE, [hi, old], low, bonus)
                then(SC, [tok, old], high, bonus)
            last["xn" + s] = tok
            while len(parts) < 2 // kk:
                yield None
            last["xT" + s + "w", count] = parts[-1]

        PARTS = ((0, 0), (1, 0), (0, 1))

        ready_q, ready_k, ready_v = {}, {}, {}
        s_last, pv_last, pv_done = {}, {}, set()

        def norm_a(ch):
            while ch not in x_tok or (ch >= 2 and ch - 2 not in v_parts):
                yield None
            yield from norm_T("A", ch, xs[ch % NX], 4, [x_tok[ch]], due(ch - 1 + AT_A - 0.15))

        v_parts = {}
        q_used = {}

        def place_q(ch, t, j, stage, d, pos):
            toks = []
            for g in (2 * t, 2 * t + 1):
                while ch and (ch - 1, g) not in q_used:
                    yield None
                after = [d, t_init, q_used.get((ch - 1, g))]
                yield SP, after, due(pos + Q_LATER * (g % 2))
                for v in range(2):
                    for h in range(4):
                        row = 64 * (g % 2) + 16 * h
                        tok = SP.dma(lambda e, g=g, v=v, h=h, row=row: e.dma_start(
                            qbd[g][64 * v + 16 * h:64 * v + 16 * h + 16, CH * h:CH * h + CH], stage[row:row + 16, v, :]), s_q[g], after)
                ready_q[ch, g] = tok
                toks.append(tok)
            qk_stage["q"].free(j, *toks)

        def place_k(ch, t, j, stage, d, pos):
            b = ch % 2
            while ch and ("kc", ch - 1) not in last:
                yield None
            after = [d, t_init, s_last.get(ch - 2), last.get(("kc", ch - 1))]
            yield SP, after, due(pos)
            for g in (2 * t, 2 * t + 1):
                for v in range(2):
                    row = 64 * (g % 2)
                    tok = SP.dma(lambda e, g=g, v=v, row=row: e.dma_start(
                        ks[b][64 * v:64 * v + 64, :, g, 64:], stage[row:row + 64, :, :]), s_k[b][t], after)
            ready_k[ch, t] = tok
            qk_stage["k"].free(j, tok)

        def carry(ch):
            b = ch % 2
            while (ch and (ch - 1, 1) not in ready_k) or (ch >= 2 and ch - 2 not in s_last):
                yield None
            after = [ready_k.get((ch - 1, 0)), ready_k.get((ch - 1, 1)), s_last.get(ch - 2), t_init]
            yield DVE, after, due(ch - 1 + AT_K)
            last["kc", ch] = DVE.do(lambda e: e.tensor_copy(
                ks[b][:, :, :, 0:64].rearrange("p v g n -> p (v g) n"),
                ks[1 - b][:, :, :, CH:CH + 64].rearrange("p v g n -> p (v g) n")), after, 200)

        def project(ch):
            b = ch % 2
            while ("xTAw", ch) not in last or not all(n in t_wt for n in "qkv") or (
                    ch >= 2 and ch - 2 not in s_last):
                yield None
            t_x = last["xTAw", ch]
            for t in range(2):
                for n in "qk":
                    pos = ch - 1 + AT_A + LEN_A * (2 * t + (n == "k")) / 6
                    while not wring.ready() or not qk_stage[n].ready():
                        yield None
                    i, bank, freed = wring.take()
                    j, stage, staged = qk_stage[n].take()
                    m = 0
                    for wp, xp in PARTS:
                        yield PE, [t_x, *freed], due(pos)
                        for k in range(2):
                            lhs = wT[n][wp][:, k, 128 * t:128 * t + 128]
                            tok = PE.do(lambda e, lhs=lhs, xp=xp, k=k, m=m, bank=bank: e.matmul(
                                bank[:, :], lhs, xT["A"][xp][:, k, :], start=(m == 0), stop=(m == 5)),
                                [t_x, t_wt[n], *freed])
                            m += 1

                    def high(n=n, t=t, bank=bank, tok=tok, i=i, j=j, stage=stage, staged=staged, at=pos):
                        hs, ls, src = stage[:, 0, :], stage[:, 1, :], bank[:, :]
                        if n == "q":
                            hs, ls = (x.rearrange("p (q a) -> p a q", a=16) for x in (hs, ls))
                            src = src.rearrange("p (a q) -> p a q", a=16)
                        a = SC.do(lambda e: e.activation(hs, src, ACT.Copy), [tok, *staged])

                        def low():
                            d = DVE.do(lambda e: e.tensor_tensor(ls, src, hs, ALU.subtract),
                                       [a, *staged])
                            wring.free(i, d)
                            spawned.append((place_q if n == "q" else place_k)(ch, t, j, stage, d, at))
                        then(DVE, [a, *staged], low, due(at))
                    then(SC, [tok, *staged], high, due(pos))
            vparts = []
            while ch and ch - 1 not in ready_v:
                yield None
            for u in range(2):
                pos = ch - 1 + AT_A + LEN_A * (4 + u) / 6
                while not wring.ready():
                    yield None
                i, bank, freed = wring.take()
                for t in range(2):
                    m = 0
                    yield PE, [t_x, *freed], due(pos)
                    for wp, xp in PARTS:
                        for k in range(2):
                            tok = PE.do(lambda e, wp=wp, xp=xp, k=k, m=m, t=t, u=u, bank=bank: e.matmul(
                                bank[:, t * 256:(t + 1) * 256],
                                xT["A"][xp][:, k, (2 * u + t) * 128:(2 * u + t + 1) * 128], wT["v"][wp][:, k, :],
                                start=(m == 0), stop=(m == 5)), [t_x, t_wt["v"], *freed], 109)
                            m += 1

                def high(u=u, bank=bank, tok=tok, i=i):
                    hi_v, lo_v = (vd[:, 2 * u:2 * u + 2, :, v].rearrange("p t g h d -> p (t g) (h d)") for v in range(2))
                    src = bank[:, :].rearrange("p (a b) -> p a b", b=64)
                    a = SC.do(lambda e: e.activation(hi_v, src, ACT.Copy), [tok, last.get("vd")])

                    def low():
                        d = DVE.do(lambda e: e.tensor_tensor(lo_v, src, hi_v, ALU.subtract), [a, last.get("vd")])
                        wring.free(i, d)
                        vparts.append(d)
                    then(DVE, [a], low, due(pos))
                then(SC, [tok], high, due(pos))
            last["xTA", ch] = tok
            while len(vparts) < 2:
                yield None
            v_parts[ch] = vparts

        def spread(ch):
            b = ch % 2
            while ch not in v_parts or ("zero", b) not in last:
                yield None
            vparts, t_init = v_parts[ch], last["zero", b]
            while ch >= 2 and (ch - 2, 3) not in pv_done:
                yield None
            pa = pv_last.get(ch - 2)
            yield DVE, [pa, *vparts, last.get("vs1")], due(ch - 1 + AT_S)
            t_c = DVE.do(lambda e: e.tensor_copy(vb[b][:, 0:2].rearrange("p c g v h d -> p (c g v h d)"),
                                                 vb[1 - b][:, 16:18].rearrange("p c g v h d -> p (c g v h d)")),
                         [pa, t_init, last.get("vs1")], 340)
            n = 0
            for c in range(4):
                for h in range(4):
                    on_dve = (n * SPREAD) // 16 != ((n + 1) * SPREAD) // 16
                    dst = vb[b][32 * h:32 * h + 32, 2 + c:18:4, :, :, h, :].rearrange("p t g v d -> p t (g v) d")
                    src = vd[32 * c:32 * c + 32, :, :, :, h, :].rearrange("p t g v d -> p t (g v) d")
                    if on_dve:
                        yield DVE, vparts, due(ch - 1 + AT_S)
                        last["vs0"] = DVE.do(lambda e, dst=dst, src=src: e.tensor_copy(dst, src), [*vparts, pa, t_init], 200)
                    else:
                        yield SC, vparts, due(ch - 1 + AT_S)
                        last["vs1"] = SC.do(lambda e, dst=dst, src=src: e.activation(dst, src, ACT.Copy),
                                            [*vparts, pa, t_init, t_c], 500)
                    n += 1
            yield DVE, [last["vs1"]], due(ch - 1 + AT_S)
            t_j = DVE.do(lambda e: e.memset(junk[:, :], 0.0), [last["vs1"]], 10)
            last["vd"] = t_j
            ready_v[ch] = t_j

        quad = {}

        def scores(n):
            ch, g, iq = n // 16, n // 4 % 4, n % 4
            while (ch, g) not in ready_q or (ch, g // 2) not in ready_k or ("kc", ch) not in last or not sring.ready():
                yield None
            i, bank, freed = sring.take()
            first = ch % PER_BATCH == 0 and iq == 0
            buf = qbd[g]
            operands = [ready_q[ch, g], ready_k[ch, g // 2], last["kc", ch]]
            yield PE, [*operands, *freed], due(n / 16) + BONUS
            PE.do(lambda e: e.matmul(bank[:, 0:384], identb[:, :], (maskf if first else mask)[:, :], start=True,
                                     stop=False, skip_group_check=True), [t_mask, *freed], 163, signal=False)
            for u in range(4):
                blk = 4 * iq + u
                for m in range(2):
                    tok = PE.do(lambda e, u=u, blk=blk, m=m: e.matmul(
                        bank[:, 96 * u:96 * u + 96], buf[:, blk::16],
                        ks[ch % 2][:, m, g, 32 * blk:32 * blk + 96], start=False, stop=(m == 1 and u == 3),
                        skip_group_check=True), operands, 43, signal=(u == 3 and m == 1))
            quad[n] = {"s": i, "bank": bank, "tok": tok}
            if iq == 3:
                q_used[ch, g] = tok
                if g == 3:
                    s_last[ch] = tok

        def softmax(n):
            while n not in quad or not (negm.ready() and pr.ready() and rsum.ready()):
                yield None
            q = quad[n]
            i, nm, freed = negm.take()
            yield DVE, [q["tok"], *freed], due(n / 16) + BONUS
            t_max = DVE.do(lambda e: e.tensor_reduce(
                nm[:, :], q["bank"][:, 0:384].rearrange("p (a b) -> p a b", b=96), AX.X, ALU.max, negate=True),
                [q["tok"], *freed], 465)
            pi, p, pf = pr.take()
            ri, r, rf = rsum.take()
            yield SC, [t_max, *pf, *rf], due(n / 16) + BONUS
            for u in range(4):
                tok = SC.do(lambda e, u=u: e.activation(
                    p[:, 96 * u:96 * u + 96], q["bank"][:, 96 * u:96 * u + 96], ACT.Exp, bias=nm[:, u:u + 1],
                    accum_out=r[:, u:u + 1]), [t_max, *pf, *rf], 317, signal=(u == 3))
            q.update(p=p, pi=pi, r=r, ri=ri, exp=tok)
            sring.free(q["s"], tok)
            negm.free(i, tok)

        def probabilities(n):
            while n not in quad or "exp" not in quad[n] or not rden.ready():
                yield None
            q = quad[n]
            i, rd, freed = rden.take()
            yield DVE, [q["exp"], *freed], due(n / 16) + BONUS
            a = DVE.do(lambda e: e.reciprocal(rd[:, :], q["r"][:, :]), [q["exp"], *freed], 94)
            rsum.free(q["ri"], a)
            p3 = q["p"][:, :].rearrange("p (a b) -> p a b", b=96)
            yield PL, [a], due(n / 16) + BONUS
            q["norm"] = PL.do(lambda e: e.tensor_tensor(
                p3, p3, rd[:, :].unsqueeze(2).to_broadcast([128, 4, 96]), ALU.mult), [a], 788)
            rden.free(i, q["norm"])

        def transposes(n):
            g, iq = n // 4, n % 4
            while n not in quad or "norm" not in quad[n] or not pt.ready():
                yield None
            q = quad[n]
            i, t, freed = pt.take()
            yield DVE, [q["norm"], *freed], due(n / 16) + BONUS
            tr = DVE.do(lambda e: e.transpose(t[:, :], q["p"][:, :]), [q["norm"], *freed], 469)
            pr.free(q["pi"], tr)
            while g >= 2 and ("pv", g - 2) not in last:
                yield None
            hi, lo = (x[g % 2][:, 384 * iq:384 * iq + 384] for x in (th, tl))
            old = last.get(("pv", g - 2))
            yield SC, [tr, old], due(n / 16) + BONUS
            a = SC.do(lambda e: e.activation(hi, t[:, :], ACT.Copy), [tr, old], 413)
            yield PL, [a, old], due(n / 16) + BONUS
            q["lo"] = PL.do(lambda e: e.tensor_tensor(lo, t[:, :], hi, ALU.subtract), [a, old], 872)
            pt.free(i, q["lo"])

        def values(gg):
            ch, g = gg // 4, gg % 4
            n = 4 * gg + 3
            while n not in quad or "lo" not in quad[n] or ch not in ready_v or not pvring.ready():
                yield None
            t_p = quad[n]["lo"]
            i, bank, freed = pvring.take()
            vbuf = vb[ch % 2]
            first = True
            for c in range(-2, 16):
                if (c + 2) % 6 == 0:
                    yield PE, [t_p, ready_v[ch], *freed], due(gg / 4 + 0.25) + BONUS_V
                i0, i1 = max(c, 0), min(c + 3, 16)
                off, k = 64 * i0 + 32 * c + 64, i1 - i0
                lhs = vbuf[:, c + 2, g].rearrange("p v h d -> p (v h d)")
                for tt in (th, tl):
                    rhs = tt[gg % 2][:, off:off + 64 * k].rearrange("p (a b) -> p a b", b=64)[:, :, 0:32]
                    tok = PE.do(lambda e, lhs=lhs, rhs=rhs, i0=i0, i1=i1, first=first, c=c: e.matmul(
                        bank[:, 32 * i0:32 * i1], lhs, rhs, start=first, stop=(c == 15), skip_group_check=True),
                        [t_p, ready_v[ch], *freed], 43)
                    first = False
            last["pv", gg] = tok
            pv_last[ch] = tok
            pv_done.add((ch, g))
            for m in range(n - 3, n + 1):
                del quad[m]
            base = 64 * (g % 2)
            dst = osum[base:base + 64, g // 2, :]
            while "bias" not in last or (ch and ("oTw", ch - 1) not in last):
                yield None
            yield SC, [tok, last.get("osum")], due(gg / 4 + 0.25) + BONUS_V
            a = SC.do(lambda e: e.activation(dst, bank[64:128, :], ACT.Copy), [tok, last.get("osum")])
            yield DVE, [a], due(gg / 4 + 0.25) + BONUS_V
            d = DVE.do(lambda e: e.tensor_tensor(dst, bank[0:64, :], dst, ALU.add), [a])
            pvring.free(i, d)
            if g % 2:
                t = g // 2
                while ch and ("wo", ch - 1) not in last:
                    yield None
                old = last.get(("wo", ch - 1))
                yield SC, [d, old], due(gg / 4 + 0.25) + BONUS_V
                hi = SC.do(lambda e: e.activation(oT[0][:, t, :], osum[:, t, :], ACT.Copy), [d, old], 520)
                eng = PL if O_LOW_POOL else DVE
                yield eng, [hi], due(gg / 4 + 0.25) + BONUS_V
                lo = eng.do(lambda e: e.tensor_tensor(
                    oT[1][:, t, :], osum[:, t, :], oT[0][:, t, :].bitcast(f32), ALU.subtract), [hi, old])
                if t == 1:
                    last["osum"] = lo
                    last["oTw", ch] = lo

        x2_ready = {}

        def residual(ch, u, bank, tok, i, ready, pos):
            x2 = xs[ch % NX][:, 2 * u:2 * u + 2, :].rearrange("p a b -> p (a b)")

            def add():
                d = DVE.do(lambda e: e.tensor_tensor(x2, bank[:, :], x2, ALU.add), [tok, *a_done[ch]])
                wring.free(i, d)
                ready[ch, u] = d
            then(DVE, [tok], add, due(pos))

        def at_c(ch):
            return ch + 1 + AT_C - (TAIL if ch == NCH - 1 else 0.0)

        def wo(ch):
            while ("oTw", ch) not in last:
                yield None
            for u in range(2):
                while not wring.ready():
                    yield None
                i, bank, freed = wring.take()
                for t in range(2):
                    m = 0
                    yield PE, [last["oTw", ch], *freed], due(at_c(ch))
                    for wp, xp in PARTS:
                        for k in range(2):
                            tok = PE.do(lambda e, wp=wp, xp=xp, k=k, m=m, t=t, u=u, bank=bank: e.matmul(
                                bank[:, t * 256:(t + 1) * 256],
                                oT[xp][:, k, (2 * u + t) * 128:(2 * u + t + 1) * 128], wT["o"][wp][:, k, :],
                                start=(m == 0), stop=(m == 5)), [last["oTw", ch], t_wt["o"], *freed], 109)
                            m += 1
                residual(ch, u, bank, tok, i, x2_ready, at_c(ch))
            last["wo", ch] = tok

        def norm_c(h):
            ch, u = h // 2, h % 2
            while (ch, u) not in x2_ready or "ffn" not in last:
                yield None
            yield from norm_T("C", h, xs[ch % NX][:, 2 * u:2 * u + 2, :], 2, [x2_ready[ch, u]], due(at_c(ch) + LEN_C * (0.1 + 0.45 * u)))

        out_ready = {}

        def ffn(h):
            ch, u = h // 2, h % 2
            while ("xTCw", h) not in last:
                yield None
            t_x, t_w = last["xTCw", h], last["ffn"]
            hparts = []
            t_oldh = last.get("hT")
            for f in range(0, 8, 2):
                pos = at_c(ch) + LEN_C * (0.2 + 0.45 * u + 0.05 * f / 2)
                while not wring.ready():
                    yield None
                i, bank, freed = wring.take()
                for j in range(2):
                    ff, o = slice((f + j) * 128, (f + j + 1) * 128), slice(j * 256, j * 256 + 256)
                    yield PE, [t_x, *freed], due(pos)
                    PE.do(lambda e, ff=ff, o=o, bank=bank: e.matmul(bank[:, o], b1p[:, ff], ones[:, 0:256],
                                                                    start=True, stop=False),
                          [last["bias"], t_ones, *freed], 109, signal=False)
                    for xp in range(2):
                        for k in range(2):
                            tok = PE.do(lambda e, ff=ff, o=o, xp=xp, k=k, bank=bank: e.matmul(
                                bank[:, o], w1T[:, k, ff], xT["C"][xp][:, k, :],
                                start=False, stop=(xp + k == 2)), [t_x, t_w], 109)

                def high(f=f, bank=bank, tok=tok, i=i):
                    hd, ld = (hT[p][:, f:f + 2, :].rearrange("p a b -> p (a b)") for p in range(2))
                    a = SC.do(lambda e: e.activation(hd, bank[:, :], ACT.Relu), [tok, t_oldh])

                    def low():
                        d = DVE.do(lambda e: e.scalar_tensor_tensor(
                            out=ld, in0=bank[:, :], scalar=0.0, in1=hd.bitcast(f32),
                            op0=ALU.max, op1=ALU.subtract), [a, t_oldh])
                        wring.free(i, d)
                        hparts.append(d)
                    then(DVE, [a, t_oldh], low, due(pos))
                then(SC, [tok, t_oldh], high, due(pos))
            last["xTC", h] = tok
            while len(hparts) < 4:
                yield None
            while not wring.ready():
                yield None
            i, bank, freed = wring.take()
            pos += 0.05 * LEN_C
            for t in range(2):
                o = slice(t * 256, (t + 1) * 256)
                yield PE, [*hparts, *freed], due(pos)
                PE.do(lambda e, o=o, bank=bank: e.matmul(bank[:, o], ones[:, 0:128], b2p[:, :], start=True, stop=False),
                      [last["bias"], t_ones, *freed], 109, signal=False)
                for f in range(8):
                    for hp in range(2):
                        tok = PE.do(lambda e, t=t, o=o, f=f, hp=hp, bank=bank: e.matmul(
                            bank[:, o], hT[hp][:, f, t * 128:(t + 1) * 128], w2T[:, f, :],
                            start=False, stop=(f == 7 and hp == 1)), [*hparts, t_w], 109)
                    if f % 2 and f < 7:
                        yield PE, [], due(pos)
            last["hT"] = tok
            residual(ch, u, bank, tok, i, out_ready, pos + 0.1)
            while (ch, u) not in out_ready:
                yield None
            if u:
                x = xs[ch % NX]
                after = [out_ready[ch, 0], out_ready[ch, 1]]
                yield SP, after
                stored = SP.dma(lambda e: e.dma_start(out_t[ch], x[:, :, :]), s_out, after)
                if ch + NX < NCH:
                    def load():
                        load_x(ch + NX, [stored])
                    then(SP, [stored], load)

        a_done = {}

        def each(stage, count):
            for n in range(count):
                yield from stage(n)

        spawned += [each(scores, NQ), each(softmax, NQ), each(probabilities, NQ), each(transposes, NQ),
                    each(values, NQ // 4), each(carry, NCH), each(wo, NCH), each(norm_c, 2 * NCH), each(ffn, 2 * NCH),
                    each(project, NCH), each(spread, NCH), each(norm_a, NCH), weights(), more_weights(), ffn_weights(), zero_values()]
        plan(spawned)
        SP.wait((s_out, 16 * NCH))

        block = ctx.enter_context(nc.Block())

        @block.sync
        def _(eng):
            SP.emit(eng)

        @block.gpsimd
        def _(eng):
            PL.emit(eng)

        @block.scalar
        def _(eng):
            SC.emit(eng)

        @block.vector
        def _(eng):
            DVE.emit(eng)

        @block.tensor
        def _(eng):
            PE.emit(eng)


_INS = ["L0_attn_hidden", "L0_attn_Wq", "L0_attn_Wk", "L0_attn_Wv", "L0_attn_Wo",
        "L0_ffn_W1", "L0_ffn_b1", "L0_ffn_W2", "L0_ffn_b2"]


def _constants():
    import numpy as np

    q = np.arange(128)[:, None, None] % 32
    u = np.arange(4)[None, :, None]
    k = np.arange(96)[None, None, :]
    seen = (k <= q + 64) & (k > q) & (u >= 0)
    inside = 32 * u - 64 + k >= 0
    mask = np.where(seen, 0.0, NEG).astype(np.float32).reshape(128, 384)
    maskf = np.where(seen & inside, 0.0, NEG).astype(np.float32).reshape(128, 384)
    return {"identf": np.eye(128, dtype=np.float32), "mask": mask, "maskf": maskf}


def kernel(**inputs):
    import numpy as np
    import concourse.bacc as bacc
    from concourse.bass_utils import run_bass_kernel_spmd

    nc = bacc.Bacc("TRN2", target_bir_lowering=False, num_devices=1)
    arrays, args = {}, []
    for name, a in [(n, inputs[n]) for n in _INS] + list(_constants().items()):
        a = np.ascontiguousarray(a)
        arrays[f"in_{name}"] = a
        args.append(nc.dram_tensor(f"in_{name}", a.shape, mybir.dt.from_np(a.dtype), kind="ExternalInput").ap())
    out = nc.dram_tensor("out", (4, 2048, 256), mybir.dt.float32, kind="ExternalOutput").ap()
    build(nc, *args, out)
    r = run_bass_kernel_spmd(nc, [arrays], core_ids=[0])
    return r.results[0]["out"]
```
